# Optimizing a Trainium2 kernel written in Bass

```python
import numpy as np
import jax
import jax.numpy as jnp

def _softmax(x, axis=-1):
    return jax.nn.softmax(x, axis=axis)

def _gelu(x):
    return jax.nn.gelu(x, approximate=True)

def _silu(x):
    return jax.nn.silu(x)

def _sigmoid(x):
    return jax.nn.sigmoid(x)

def _layernorm(x, axis=-1, eps=1e-05):
    m = jnp.mean(x, axis=axis, keepdims=True)
    v = jnp.var(x, axis=axis, keepdims=True)
    return (x - m) / jnp.sqrt(v + eps)

def _scatter_add(tgt, idx, src, axis=0):
    return tgt.at[idx].add(src)

def _segment_sum(src, seg, n):
    return jax.ops.segment_sum(src, seg, n)
kernel_name = 'mk_adaln_attn_ffn_d1_seqx_r8_00fdb7'

def setup_inputs(seed: int=0):
    np.random.seed(seed)
    _w = jnp.asarray

    def _rec_inputs():
        import jax
        import jax.numpy as jnp
        _rk = jax.random.key(seed)
        x = -7.109e-05 + 0.9999 * jax.random.normal(jax.random.fold_in(_rk, 1), (16, 128, 256), jnp.float32)
        _lenS = 128 - jax.random.randint(jax.random.fold_in(_rk, 7), (16,), 0, max(1, 128 // 4) + 1, jnp.int32)
        _lenS2 = 128 - jax.random.randint(jax.random.fold_in(_rk, 8), (16,), 0, max(1, 128 // 4) + 1, jnp.int32)
        itok_B_0_6 = jax.random.randint(jax.random.fold_in(_rk, 11), (16,), 0, 7, jnp.int32)
        itok_B_0_15 = jax.random.randint(jax.random.fold_in(_rk, 12), (16,), 0, 16, jnp.int32)
        return (x, itok_B_0_6, itok_B_0_15)
    x, itok_B_0_6, itok_B_0_15 = _rec_inputs()

    def _L0_cond_setup():
        import jax, jax.numpy as jnp
        import numpy as np
        B, T, D_IN, D_OUT = (16, 256, 256, 256)
        N_ADAPTERS, RANK = (8, 16)
        key = jax.random.key(seed)
        k_x, k_w, k_a, k_b, k_s, k_idx = jax.random.split(key, 6)
        x = jax.random.normal(k_x, (B, T, D_IN), dtype=jnp.float32)
        W = jax.random.normal(k_w, (D_OUT, D_IN), dtype=jnp.float32) * (1.0 / np.sqrt(D_IN))
        A = jax.random.normal(k_a, (N_ADAPTERS, RANK, D_IN), dtype=jnp.float32) * 0.02
        Bm = jax.random.normal(k_b, (N_ADAPTERS, D_OUT, RANK), dtype=jnp.float32) * 0.02
        scalings = jnp.ones((N_ADAPTERS,), dtype=jnp.float32)
        adapter_idx = jax.random.randint(k_idx, (B,), 0, N_ADAPTERS, dtype=jnp.int32)
        return {'x': x, 'W': W, 'A': A, 'Bm': Bm, 'scalings': scalings, 'adapter_idx': adapter_idx}
    _L0_cond_all = _L0_cond_setup()
    _L0_cond_in = {k: v for k, v in _L0_cond_all.items() if k in ('W', 'A', 'Bm', 'scalings')}
    del _L0_cond_all

    def _L0_attn_setup():
        import jax, jax.numpy as jnp
        import numpy as np
        N_HEAD = 16
        key = jax.random.key(seed)
        ks = jax.random.split(key, 9)
        H = 256

        def w(k, shape, scale=0.02):
            return jax.random.normal(k, shape, dtype=jnp.float32) * scale
        return {'h': jax.random.normal(ks[0], (4, 256, H), dtype=jnp.float32), 'Wq': w(ks[1], (H, H)), 'bq': w(ks[2], (H,)), 'Wk': w(ks[3], (H, H)), 'bk': w(ks[4], (H,)), 'Wv': w(ks[5], (H, H)), 'bv': w(ks[6], (H,)), 'Wo': w(ks[7], (H, H)), 'bo': w(ks[8], (H,))}
    _L0_attn_all = _L0_attn_setup()
    _L0_attn_in = {k: v for k, v in _L0_attn_all.items() if k in ('Wq', 'bq', 'Wk', 'bk', 'Wv', 'bv', 'Wo', 'bo')}
    del _L0_attn_all

    def _L0_cond2_setup():
        import jax, jax.numpy as jnp
        import numpy as np
        key = jax.random.key(seed)
        k1, k2, k3, k4 = jax.random.split(key, 4)
        B, S, IN, OUT, E = (64, 32, 256, 256, 16)
        bound = 1.0 / np.sqrt(IN)
        x = jax.random.normal(k1, (B, S, IN), dtype=jnp.float32)
        idx = jax.random.randint(k2, (B,), 0, E, dtype=jnp.int64)
        W = jax.random.uniform(k3, (E, IN, OUT), dtype=jnp.float32, minval=-bound, maxval=bound)
        b = jnp.full((E, OUT), 0.1, dtype=jnp.float32)
        return {'x': x, 'id': idx, 'W': W, 'b': b}
    _L0_cond2_all = _L0_cond2_setup()
    _L0_cond2_in = {k: v for k, v in _L0_cond2_all.items() if k in ('W', 'b')}
    del _L0_cond2_all

    def _L0_ffn_setup():
        import jax, jax.numpy as jnp
        import numpy as np
        ALPHA = 1.702
        LIMIT = 7.0
        TOP_K = 4
        B, S, H = (1, 128, 256)
        E, D = (16, 256)
        key = jax.random.key(seed)
        ks = jax.random.split(key, 7)
        s = 0.02
        return {'hidden_states': jax.random.normal(ks[0], (B, S, H), dtype=jnp.float32), 'router_weight': jax.random.normal(ks[1], (E, H), dtype=jnp.float32) * s, 'router_bias': jax.random.normal(ks[2], (E,), dtype=jnp.float32) * s, 'gate_up_proj': jax.random.normal(ks[3], (E, H, 2 * D), dtype=jnp.float32) * s, 'gate_up_proj_bias': jax.random.normal(ks[4], (E, 2 * D), dtype=jnp.float32) * s, 'down_proj': jax.random.normal(ks[5], (E, D, H), dtype=jnp.float32) * s, 'down_proj_bias': jax.random.normal(ks[6], (E, H), dtype=jnp.float32) * s}
    _L0_ffn_all = _L0_ffn_setup()
    _L0_ffn_in = {k: v for k, v in _L0_ffn_all.items() if k in ('router_weight', 'router_bias', 'gate_up_proj', 'gate_up_proj_bias', 'down_proj', 'down_proj_bias')}
    del _L0_ffn_all
    return {'x': x, 'itok_B_0_6': itok_B_0_6, 'itok_B_0_15': itok_B_0_15, 'L0_cond_W': _L0_cond_in['W'], 'L0_cond_A': _L0_cond_in['A'], 'L0_cond_Bm': _L0_cond_in['Bm'], 'L0_cond_scalings': _L0_cond_in['scalings'], 'L0_attn_Wq': _L0_attn_in['Wq'], 'L0_attn_bq': _L0_attn_in['bq'], 'L0_attn_Wk': _L0_attn_in['Wk'], 'L0_attn_bk': _L0_attn_in['bk'], 'L0_attn_Wv': _L0_attn_in['Wv'], 'L0_attn_bv': _L0_attn_in['bv'], 'L0_attn_Wo': _L0_attn_in['Wo'], 'L0_attn_bo': _L0_attn_in['bo'], 'L0_cond2_W': _L0_cond2_in['W'], 'L0_cond2_b': _L0_cond2_in['b'], 'L0_ffn_router_weight': _L0_ffn_in['router_weight'], 'L0_ffn_router_bias': _L0_ffn_in['router_bias'], 'L0_ffn_gate_up_proj': _L0_ffn_in['gate_up_proj'], 'L0_ffn_gate_up_proj_bias': _L0_ffn_in['gate_up_proj_bias'], 'L0_ffn_down_proj': _L0_ffn_in['down_proj'], 'L0_ffn_down_proj_bias': _L0_ffn_in['down_proj_bias']}

def reference(x, itok_B_0_6, itok_B_0_15, L0_cond_W, L0_cond_A, L0_cond_Bm, L0_cond_scalings, L0_attn_Wq, L0_attn_bq, L0_attn_Wk, L0_attn_bk, L0_attn_Wv, L0_attn_bv, L0_attn_Wo, L0_attn_bo, L0_cond2_W, L0_cond2_b, L0_ffn_router_weight, L0_ffn_router_bias, L0_ffn_gate_up_proj, L0_ffn_gate_up_proj_bias, L0_ffn_down_proj, L0_ffn_down_proj_bias):
    import jax
    import jax.numpy as jnp

    def _L0_cond_ref(x, W, A, Bm, scalings, adapter_idx):
        import jax, jax.numpy as jnp
        import numpy as np
        B, T, D_IN, D_OUT = (16, 256, 256, 256)
        N_ADAPTERS, RANK = (8, 16)
        H = jnp.einsum('btd,od->bto', x, W)
        A_b = A[adapter_idx]
        B_b = Bm[adapter_idx]
        s_b = scalings[adapter_idx]
        xa = jnp.einsum('btd,brd->btr', x, A_b)
        delta = jnp.einsum('btr,bor->bto', xa, B_b)
        delta = jax.lax.stop_gradient(delta * s_b[:, None, None])
        return H + delta

    def _L0_attn_ref(h, Wq, bq, Wk, bk, Wv, bv, Wo, bo):
        import jax, jax.numpy as jnp
        import numpy as np
        N_HEAD = 16
        B, S, H = h.shape
        nh = N_HEAD
        hd = H // nh
        q = (h @ Wq.T + bq).reshape(B, S, nh, hd)
        k = (h @ Wk.T + bk).reshape(B, S, nh, hd)
        v = (h @ Wv.T + bv).reshape(B, S, nh, hd)
        scale = 1.0 / jnp.sqrt(jnp.float32(hd))
        scores = jnp.einsum('bqhd,bkhd->bhqk', q, k) * scale
        causal = jnp.tril(jnp.ones((S, S), dtype=bool))
        scores = jnp.where(causal, scores, jnp.finfo(scores.dtype).min)
        attn = jax.nn.softmax(scores, axis=-1)
        o = jnp.einsum('bhqk,bkhd->bqhd', attn, v).reshape(B, S, H)
        return o @ Wo.T + bo

    def _L0_cond2_ref(x, id, W, b):
        import jax, jax.numpy as jnp
        import numpy as np
        Wg = W[id]
        bg = b[id]
        out = jnp.einsum('bsi,bio->bso', x, Wg) + bg[:, None, :]
        return out

    def _L0_ffn_ref(hidden_states, router_weight, router_bias, gate_up_proj, gate_up_proj_bias, down_proj, down_proj_bias):
        import jax, jax.numpy as jnp
        import numpy as np
        ALPHA = 1.702
        LIMIT = 7.0
        TOP_K = 4
        B, S, H = (1, 128, 256)
        E, D = (16, 256)
        batch, seq, hdim = hidden_states.shape
        x = hidden_states.reshape(-1, hdim)
        T = x.shape[0]
        logits = x @ router_weight.T + router_bias
        top_val, top_idx = jax.lax.top_k(logits, TOP_K)
        top_val = jax.nn.softmax(top_val, axis=-1)
        router_scores = jnp.zeros_like(logits).at[jnp.arange(T)[:, None], top_idx].set(top_val)
        gate_up = jnp.einsum('th,ehd->etd', x, gate_up_proj) + gate_up_proj_bias[:, None, :]
        gate = gate_up[..., ::2]
        up = gate_up[..., 1::2]
        gate = jnp.minimum(gate, LIMIT)
        up = jnp.clip(up, -LIMIT, LIMIT)
        glu = gate * jax.nn.sigmoid(gate * ALPHA)
        out = jnp.einsum('etd,edh->eth', (up + 1.0) * glu, down_proj) + down_proj_bias[:, None, :]
        out = out * router_scores.T[:, :, None]
        out = out.sum(axis=0)
        return out.reshape(batch, seq, hdim)
    x = x + _L0_attn_ref(_L0_cond_ref(x, L0_cond_W, L0_cond_A, L0_cond_Bm, L0_cond_scalings, itok_B_0_6), L0_attn_Wq, L0_attn_bq, L0_attn_Wk, L0_attn_bk, L0_attn_Wv, L0_attn_bv, L0_attn_Wo, L0_attn_bo)
    x = x + _L0_ffn_ref(_L0_cond2_ref(x, itok_B_0_15, L0_cond2_W, L0_cond2_b), L0_ffn_router_weight, L0_ffn_router_bias, L0_ffn_gate_up_proj, L0_ffn_gate_up_proj_bias, L0_ffn_down_proj, L0_ffn_down_proj_bias)
    return x

_drawn_inputs = setup_inputs


def setup_inputs(seed=0):
    import zlib

    import numpy as np

    out = dict(_drawn_inputs(seed))
    spreads = {'L0_cond_scalings': (1.0, 0.6), 'L0_cond2_b': (0.10000000149011612, 0.6)}
    factors = {'L0_cond_A': 8.0,
     'L0_cond_Bm': 8.0,
     'L0_attn_Wq': 8.0,
     'L0_attn_bq': 8.0,
     'L0_attn_Wk': 8.0,
     'L0_attn_bk': 8.0,
     'L0_attn_bv': 8.0,
     'L0_attn_bo': 2.932,
     'L0_cond2_W': 3.136,
     'L0_ffn_router_weight': 3.459,
     'L0_ffn_router_bias': 8.0,
     'L0_ffn_gate_up_proj': 3.603,
     'L0_ffn_gate_up_proj_bias': 8.0,
     'L0_ffn_down_proj': 3.537,
     'L0_ffn_down_proj_bias': 5.678}
    for name, (base, spread) in spreads.items():
        noise = np.random.default_rng([zlib.crc32(name.encode()), seed]).standard_normal(out[name].shape)
        drawn = base * np.exp(spread * noise) if base else spread * noise
        out[name] = jnp.asarray(drawn.astype(out[name].dtype))
    for name, factor in factors.items():
        out[name] = (out[name] * factor).astype(out[name].dtype)
    return out
```

```python
import concourse.bass as bass
from concourse import mybir
from contextlib import ExitStack

F32 = mybir.dt.float32
BF16 = mybir.dt.bfloat16
I32 = mybir.dt.int32
U32 = mybir.dt.uint32
ALU = mybir.AluOpType
ACT = mybir.ActivationFunctionType
AX = mybir.AxisListType

B = 16
S = 128
H = 256
C = H // 128
NH = 16
HD = H // NH
G = 4
GH = NH // G
RANK = 16
E = 16
D = 256
TOPK = 4
ALPHA = 1.702
LIMIT = 7.0
ROWS = B * S
NT = ROWS * TOPK // 128 + E - 1 + 1
RT = ROWS // 128
TCOLS = E * RT + 1
PADROWS = 128


def adaln_attn_moe(nc: bass.Bass, a, out):
    ctx = ExitStack()
    with ctx:
        def sb(name, shape, dt=F32):
            return ctx.enter_context(nc.sbuf_tensor(name, shape, dt))

        def ps(name, dt=F32):
            return ctx.enter_context(nc.psum_tensor(name, [128, 512], dt))

        def sem(name):
            return ctx.enter_context(nc.semaphore(name))

        x2_rows = nc.dram_tensor("x2_rows", [ROWS + PADROWS, H], F32, kind="Internal").ap()
        slot_table = nc.dram_tensor("slot_table", [128 * TCOLS, 2], I32, kind="Internal").ap()
        table_by_row = slot_table.rearrange("(p c) two -> p (c two)", c=TCOLS)

        ident = sb("ident", [128, 128])
        identb = sb("identb", [128, 128], BF16)
        causal = sb("causal", [128, GH * 128], BF16)
        tri = sb("tri", [128, 128], BF16)
        onesb = sb("onesb", [128, 128], BF16)
        iota_e = sb("iota_e", [128, E])
        ebase = sb("ebase", [128, E])
        iota_t = sb("iota_t", [1, NT])
        kmask = sb("kmask", [128, 2])
        idx = sb("idx", [1, 2 * B], I32)
        WT = sb("WT", [128, C, H])
        WqT = sb("WqT", [128, C, H])
        WkT = sb("WkT", [128, C, H])
        WvT = sb("WvT", [128, C, H])
        WoT = sb("WoT", [128, C, H])
        RWT = sb("RWT", [128, C, E])
        bq = sb("bq", [128, C])
        bk = sb("bk", [128, C])
        bv = sb("bv", [128, H])
        bo = sb("bo", [128, H])
        rbias = sb("rbias", [128, E])

        xT = [sb(f"xT{i}", [128, C, S]) for i in range(2)]
        AT = [sb(f"AT{i}", [128, C, RANK]) for i in range(2)]
        BT = [sb(f"BT{i}", [RANK, H]) for i in range(2)]
        scal = [sb(f"scal{i}", [RANK, 1]) for i in range(2)]
        xrow = [sb(f"xrow{i}", [S, H]) for i in range(2)]
        W2 = [sb(f"W2_{i}", [128, C, H]) for i in range(2)]
        b2 = [sb(f"b2_{i}", [S, H]) for i in range(2)]
        xa = sb("xa", [RANK, S])
        hT = sb("hT", [128, C, S])
        qT = sb("qT", [128, C, S])
        kM = sb("kM", [128, C, 2, S])
        vaug = [sb(f"vaug{i}", [S, NH, HD + 1]) for i in range(2)]
        P = sb("P", [S, G, GH, S])
        nmax = sb("nmax", [S, G, GH])
        PT = [sb(f"PT{i}", [S, GH, S]) for i in range(2)]
        rsum = sb("rsum", [S, 2, GH])
        o = sb("o", [S, NH, HD])
        oT = sb("oT", [128, C, S])
        xb = sb("xb", [S, H])
        x1 = [sb(f"x1_{i}", [S, H]) for i in range(2)]
        x1T = sb("x1T", [128, C, S])
        x2 = [sb(f"x2_{i}", [S, H]) for i in range(2)]
        x2T = sb("x2T", [128, C, S])
        lg = sb("lg", [S, E])
        top8 = sb("top8", [S, 8])
        topi = sb("topi", [S, 8], U32)
        topf = sb("topf", [S, TOPK])
        onehot = sb("onehot", [S, TOPK, E])
        sel = sb("sel", [S, E], BF16)
        selsum = sb("selsum", [S, E], BF16)
        rank = sb("rank", [S, E])
        prod = sb("prod", [S, TOPK, E])
        slot = sb("slot", [S, TOPK], I32)
        slot_p = sb("slot_p", [S, TOPK], I32)
        slot_c = sb("slot_c", [S, TOPK], I32)
        slot_row = [sb(f"slot_row{i}", [S, TOPK], I32) for i in range(2)]
        pair = [sb(f"pair{i}", [S, TOPK, 2], I32) for i in range(2)]
        dtop = sb("dtop", [S, TOPK])
        etop = sb("etop", [S, TOPK])
        esum = sb("esum", [S, 1])
        einv = sb("einv", [S, 1])

        Wgu = sb("Wgu", [128, E * C * 2 * D])
        Wd = sb("Wd", [128, E * C * H])
        bgu = sb("bgu", [128, E * 2 * D])
        bd = sb("bd", [128, E * H])
        table = sb("table", [128, TCOLS * 2], I32)
        zrow = sb("zrow", [128, H])

        cnt = sb("cnt", [1, E], I32)
        ntile = sb("ntile", [1, E], I32)
        ntilef = sb("ntilef", [1, E])
        cum = sb("cum", [1, E])
        one_e = sb("one_e", [1, E])
        past = P[0:1].rearrange("p g h s -> p (g h s)")[:, 0:NT * E].rearrange("p (t e) -> p t e", e=E)
        t_e = sb("t_e", [1, NT])
        t_s = sb("t_s", [1, NT])
        t_r = sb("t_r", [1, NT])
        tile_e = sb("tile_e", [1, NT], I32)
        tile_c = sb("tile_c", [1, NT], I32)

        idg = [sb(f"idg{i}", [128, 2], I32) for i in range(2)]
        ids = [sb(f"ids{i}", [128, 2], I32) for i in range(2)]
        def halves(t):
            w = t[:].rearrange("p c n -> p (c n)")
            return [w[:, 0:H], w[:, H:2 * H]]

        xg = halves(WvT)
        xgT = halves(PT[0])
        gu = [P[:, 2 + i].rearrange("p h s -> p (h s)").rearrange("p (k d) -> p k d", k=2) for i in range(2)]
        hhT = halves(PT[1])
        hh = halves(W2[0])
        sg = halves(W2[1])
        yb = halves(WqT)
        yw = halves(WkT)

        bank = [ps(f"bank{i}") for i in range(8)]
        SC = bank[0:4]
        PB = bank[4:6]
        M = bank[6:8]
        GU = bank[0:2]
        XTB = bank[2:4]
        HTB = bank[4:6]
        YB = bank[6:8]

        s_const = sem("const_loaded")
        s_idx = sem("idx_loaded")
        s_early = [sem(f"early_loaded{i}") for i in range(2)]
        s_late = [sem(f"late_loaded{i}") for i in range(2)]
        s_experts = sem("experts_loaded")
        s_init = sem("init_done")
        s_tinit = sem("table_init_stored")
        names = ("xa_ready xa_done h_ready h_done q_ready q_done k_ready k_done v_ready v_done scores_ready "
                 "max_done sub_done exp_done pt_ready pt_done pv_ready rsum_done norm_done oT_ready oT_done "
                 "x1_ready x1_done x1T_ready x1T_done x2_ready x2_done x2T_ready x2T_done lg_ready lg_done "
                 "xb_done top_done topi_done topf_done onehot_done sel_done rank_ready rank_done prod_done "
                 "slot_done slotp_done slotc_done slotrow_done dtop_done etop_done esum_done einv_done "
                 "pair_done selsum_done").split()
        z = {n: sem(n) for n in names}
        s_x1_stored = [sem(f"x1_stored{i}") for i in range(2)]
        s_x2_stored = [sem(f"x2_stored{i}") for i in range(2)]
        s_scattered = [sem(f"pairs_scattered{i}") for i in range(2)]
        s_pad = sem("pad_rows_stored")
        s_passed = sem("waits_passed")
        s_cnt = sem("counts_ready")
        s_plan = sem("plan_steps")
        s_table = sem("table_loaded")
        s_gathered = [sem(f"rows_gathered{i}") for i in range(2)]
        s_added = sem("rows_added")
        names = ("idg_done ids_done xgT_ready xgT_done gu_ready gub_done gclip_done uclip_done sig_done glu_done "
                 "hh_done hhT_ready hhT_done y_ready yb_done yw_done").split()
        f = {n: sem(n) for n in names}

        def wait(eng, s, value):
            if not isinstance(value, int) or value > 0:
                eng.wait_ge(s, value)

        def stand_alone(eng, *waits):
            for s, v in waits:
                wait(eng, s, v)
            eng.sem_inc(s_passed, 1)

        def steps(eng, lo, hi, full_lo, full_hi, body):
            for t in range(lo, full_lo):
                body(t, t % 2, t // 2)
            with eng.Fori(0, (full_hi - full_lo) // 2) as j:
                for u in range(2):
                    body(j * 2 + (full_lo + u), (full_lo + u) % 2, j + (full_lo + u) // 2)
            for t in range(full_hi, hi):
                body(t, t % 2, t // 2)

        def within(t, off, n=B):
            return not isinstance(t, int) or 0 <= t + off < n

        def group_heads(ap, g):
            return ap.rearrange("q (c g p) d -> q g c p d", c=C, g=G)[:, g]

        block = ctx.enter_context(nc.Block())

        CONSTS = ((ident, "ident"), (identb, "identb"), (causal, "causal"), (tri, "tri"), (onesb, "onesb"),
                  (iota_e, "iota_e"), (ebase, "ebase"), (iota_t, "iota_t"), (kmask, "kmask"), (WT, "WT"), (WqT, "WqT"),
                  (WkT, "WkT"), (WvT, "WvT"), (WoT, "WoT"), (RWT, "RWT"), (bq, "bq"), (bk, "bk"), (bv, "bv"),
                  (bo, "bo"), (rbias, "rbias"), (table, "table"), (pair[0], "pair0"), (pair[1], "pair1"))

        @block.sync
        def _(sp):
            sp.dma_start(idx[:, :], a["idx"]).then_inc(s_idx, 16)
            for dst, name in CONSTS:
                src = a[name].partition_broadcast(128) if name in ("bv", "bo", "rbias") else a[name]
                sp.dma_start(dst[:], src).then_inc(s_const, 16)
            sp.wait_ge(s_idx, 16)

            def early(b, par, half):
                wait(sp, z["h_ready"], b - 1)
                ad = sp.value_load(idx[0:1, bass.ds(b, 1)], min_val=0, max_val=7)
                sp.dma_start(xT[par][:], a["xT"][bass.ds(b, 1)].rearrange("o p c t -> (o p) c t")).then_inc(s_early[par], 16)
                sp.dma_start(AT[par][:], a["AT"][bass.ds(ad, 1)].rearrange("o p c r -> (o p) c r")).then_inc(s_early[par], 16)
                sp.dma_start(BT[par][:], a["BT"][bass.ds(ad, 1)].rearrange("o r h -> (o r) h")).then_inc(s_early[par], 16)
                sp.dma_start(scal[par][:], a["scal"][bass.ds(ad, 1)].partition_broadcast(RANK)).then_inc(s_early[par], 16)

            def late(b, par, half):
                wait(sp, z["x2_done"], b - 1)
                wait(sp, z["xb_done"], b - 1)
                ex = sp.value_load(idx[0:1, bass.ds(b + B, 1)], min_val=0, max_val=E - 1)
                sp.dma_start(xrow[par][:], a["x"][bass.ds(b, 1)].rearrange("o t h -> (o t) h")).then_inc(s_late[par], 16)
                sp.dma_start(W2[par][:], a["W2"][bass.ds(ex, 1)].rearrange("o p c h -> (o p) c h")).then_inc(s_late[par], 16)
                sp.dma_start(b2[par][:], a["b2"][bass.ds(ex, 1)].rearrange("o h -> (o h)").partition_broadcast(S)).then_inc(s_late[par], 16)

            def store(b, par, half):
                wait(sp, z["x1_done"], b + 1)
                sp.dma_start(out[bass.ds(b * S, S)], x1[par][:]).then_inc(s_x1_stored[par], 16)
                wait(sp, z["x2_done"], b + 1)
                sp.dma_start(x2_rows[bass.ds(b * S, S)], x2[par][:]).then_inc(s_x2_stored[par], 16)

            early(0, 0, 0)
            early(1, 1, 0)
            late(0, 0, 0)
            sp.wait_ge(s_const, 16 * len(CONSTS))
            sp.dma_start(table_by_row, table[:, :]).then_inc(s_tinit, 16)
            sp.wait_ge(s_init, 1)
            sp.dma_start(x2_rows[ROWS:ROWS + PADROWS], zrow[:]).then_inc(s_pad, 16)
            sp.dma_start(out[ROWS:ROWS + PADROWS], zrow[:]).then_inc(s_pad, 16)

            def step(i, par, half):
                if within(i, 2):
                    early(i + 2, par, half + 1)
                if within(i, -1):
                    store(i - 1, 1 - par, half if par else half - 1)
                if within(i, 1):
                    late(i + 1, 1 - par, half + 1 if par else half)
                if isinstance(i, int) and i == 0:
                    for e in range(0, E, 4):
                        sp.dma_start(Wgu[:, e * C * 2 * D:(e + 4) * C * 2 * D],
                                     a["Wgu"][:, e * C * 2 * D:(e + 4) * C * 2 * D]).then_inc(s_experts, 16)
                        sp.dma_start(Wd[:, e * C * H:(e + 4) * C * H],
                                     a["Wd"][:, e * C * H:(e + 4) * C * H]).then_inc(s_experts, 16)
                    sp.dma_start(bgu[:], a["bgu"].partition_broadcast(128)).then_inc(s_experts, 16)
                    sp.dma_start(bd[:], a["bd"].partition_broadcast(128)).then_inc(s_experts, 16)

            steps(sp, 0, B + 1, 1, 13, step)

            for par in range(2):
                sp.wait_ge(s_scattered[par], 16 * TOPK * (B // 2))
            sp.dma_start(table[:, :], table_by_row).then_inc(s_table, 16)
            sp.wait_ge(s_added, 16 * NT)

        @block.gpsimd
        def _(pool):
            pool.memset(zrow[:], 0.0).then_inc(s_init, 1)
            pool.wait_ge(s_const, 16 * len(CONSTS))

            def step(i, par, half):
                b, bp, bh = i - 1, 1 - par, (half if par else half - 1)
                wait(pool, s_late[bp], (bh + 1) * 48)
                wait(pool, z["x1_done"], b)
                pool.tensor_tensor(out=xb[:], in0=xrow[bp][:], in1=bo[:], op=ALU.add).then_inc(z["xb_done"], 1)
                stand_alone(pool, (z["slotrow_done"], b + 1), (z["pair_done"], b + 1))
                if isinstance(i, int) and i == 1:
                    pool.wait_ge(s_tinit, 16)
                for j in range(TOPK):
                    pool.indirect_dma_start(
                        out=slot_table, out_offset=bass.IndirectOffsetOnAxis(ap=slot_row[bp][:, j:j + 1], axis=0),
                        in_=pair[bp][:, j, :], in_offset=None).then_inc(s_scattered[bp], 16)

            steps(pool, 1, B + 1, 3, B + 1, step)

            pool.wait_ge(s_table, 16)
            pool.wait_ge(s_plan, PLAN)
            for par in range(2):
                pool.wait_ge(s_x2_stored[par], 16 * (B // 2))
                pool.wait_ge(s_x1_stored[par], 16 * (B // 2))
            pool.wait_ge(s_pad, 32)

            def gather(t, par, half):
                c = pool.value_load(tile_c[0:1, bass.ds(t, 1)], min_val=0, max_val=TCOLS - 1)
                wait(pool, s_gathered[par], half * 16)
                pool.tensor_copy(idg[par][:], table[:, bass.ds(c * 2, 2)]).then_inc(f["idg_done"], 1)
                stand_alone(pool, (f["idg_done"], t + 1), (f["xgT_ready"], t - 1))
                pool.indirect_dma_start(
                    out=xg[par][:], out_offset=None, in_=x2_rows,
                    in_offset=bass.IndirectOffsetOnAxis(ap=idg[par][:, 0:1], axis=0)).then_inc(s_gathered[par], 16)

            def add(t, par, half):
                stand_alone(pool, (f["yw_done"], t + 1), (s_added, t * 16))
                pool.indirect_dma_start(
                    out=out, out_offset=bass.IndirectOffsetOnAxis(ap=ids[par][:, 0:1], axis=0),
                    in_=yw[par][:], in_offset=None, compute_op=ALU.add).then_inc(s_added, 16)

            def keep(t, par, half):
                c = pool.value_load(tile_c[0:1, bass.ds(t, 1)], min_val=0, max_val=TCOLS - 1)
                wait(pool, s_added, (t - 1) * 16)
                pool.tensor_copy(ids[par][:], table[:, bass.ds(c * 2, 2)]).then_inc(f["ids_done"], 1)

            for t in range(2):
                gather(t, t % 2, t // 2)

            def tstep(t, par, half):
                if within(t, 2, NT):
                    gather(t + 2, par, half + 1)
                if within(t, -3, NT):
                    add(t - 3, 1 - par, half - 1 if par else half - 2)
                if within(t, -2, NT):
                    keep(t - 2, par, half - 1)

            steps(pool, 0, NT + 3, 4, NT - 2, tstep)

        @block.tensor
        def _(pe):
            pe.wait_ge(s_const, 16 * len(CONSTS))

            def t_o(b):
                wait(pe, z["norm_done"], b * G + G)
                wait(pe, z["lg_done"], b)
                of = o[:].rearrange("q h d -> q (h d)")
                for c in range(C):
                    m = pe.transpose(M[0][:, c * S:(c + 1) * S], of[:, c * 128:(c + 1) * 128], ident[:])
                m.then_inc(z["oT_ready"], 1)

            def t_wo(b, v_before):
                wait(pe, z["oT_done"], b + 1)
                wait(pe, z["rank_done"], b)
                wait(pe, z["v_done"], v_before)
                for c in range(C):
                    m = pe.matmul(M[1][:, 0:H], oT[:, c, :], WoT[:, c, :], start=(c == 0), stop=(c == C - 1))
                m.then_inc(z["x1_ready"], 1)

            def t_x1T(b, par):
                wait(pe, z["x1_done"], b + 1)
                wait(pe, z["xa_done"], b + 1)
                for c in range(C):
                    m = pe.transpose(M[0][:, c * S:(c + 1) * S], x1[par][:, c * 128:(c + 1) * 128], ident[:])
                m.then_inc(z["x1T_ready"], 1)

            def t_w2(b, par, half):
                wait(pe, s_late[par], (half + 1) * 48)
                wait(pe, z["x1T_done"], b + 1)
                for c in range(C):
                    m = pe.matmul(M[0][:, 0:H], x1T[:, c, :], W2[par][:, c, :], start=(c == 0), stop=(c == C - 1))
                m.then_inc(z["x2_ready"], 1)

            def t_x2T(b, par):
                wait(pe, z["x2_done"], b + 1)
                for c in range(C):
                    m = pe.transpose(M[0][:, c * S:(c + 1) * S], x2[par][:, c * 128:(c + 1) * 128], ident[:])
                m.then_inc(z["x2T_ready"], 1)

            def t_lg(b):
                wait(pe, z["x2T_done"], b + 1)
                for c in range(C):
                    m = pe.matmul(M[0][:, 0:E], x2T[:, c, :], RWT[:, c, :], start=(c == 0), stop=(c == C - 1))
                m.then_inc(z["lg_ready"], 1)

            def t_rank(b, v_before):
                wait(pe, z["sel_done"], b + 1)
                wait(pe, z["selsum_done"], b + 1)
                wait(pe, z["v_done"], v_before)
                pe.matmul(M[1][:, 0:E], tri[:], sel[:], start=True, stop=False)
                pe.matmul(M[1][:, 0:E], onesb[:], selsum[:], start=False, stop=True).then_inc(z["rank_ready"], 1)

            def p_xa(b, par, half):
                wait(pe, s_early[par], (half + 1) * 64)
                wait(pe, z["oT_done"], b - 1)
                wait(pe, z["lg_done"], b - 2)
                for c in range(C):
                    m = pe.matmul(M[0][0:RANK, 0:S], AT[par][:, c, :], xT[par][:, c, :], start=(c == 0), stop=(c == C - 1))
                m.then_inc(z["xa_ready"], 1)

            def p_h(b, par):
                wait(pe, z["xa_done"], b + 1)
                wait(pe, z["x1_done"], b - 1)
                wait(pe, z["v_done"], b)
                for k in range(C):
                    dst = M[1][:, k * S:(k + 1) * S]
                    for c in range(C):
                        pe.matmul(dst, WT[:, c, k * 128:(k + 1) * 128], xT[par][:, c, :], start=(c == 0), stop=False)
                    m = pe.matmul(dst, BT[par][:, k * 128:(k + 1) * 128], xa[:], start=False, stop=True)
                m.then_inc(z["h_ready"], 1)

            def p_qk(b, w, ready):
                for k in range(C):
                    for c in range(C):
                        m = pe.matmul(M[1][:, k * S:(k + 1) * S], w[:, c, k * 128:(k + 1) * 128], hT[:, c, :],
                                      start=(c == 0), stop=(c == C - 1))
                m.then_inc(z[ready], 1)

            def p_v(b):
                wait(pe, z["k_done"], b * 2 + 2)
                for c in range(C):
                    m = pe.matmul(M[1][:, 0:H], hT[:, c, :], WvT[:, c, :], start=(c == 0), stop=(c == C - 1))
                m.then_inc(z["v_ready"], 1)

            def scores(b):
                wait(pe, z["sub_done"], b * G)
                for g in range(G):
                    pe.matmul(SC[g][:], identb[:], causal[:], start=True, stop=True)
                wait(pe, z["q_done"], b + 1)
                wait(pe, z["k_done"], b * 2 + 2)
                for c in range(C):
                    for g in range(G):
                        m = pe.matmul(SC[g][:, c * 256:(c + 1) * 256], qT[32 * g:32 * g + 32, c, :],
                                      kM[32 * g:32 * g + 32, c, :, :].rearrange("p e t -> p (e t)"),
                                      start=False, stop=True, skip_group_check=True)
                        if c == C - 1:
                            m.then_inc(z["scores_ready"], 1)

            def transp(b, g):
                wait(pe, z["exp_done"], b * G + (g + 1))
                wait(pe, z["norm_done"], b * G + (g - 1))
                for n in range(GH):
                    m = pe.transpose(PB[g % 2][:, n * S:(n + 1) * S], P[:, g, n, :], ident[:])
                m.then_inc(z["pt_ready"], 1)

            def pv(b, g, par):
                wait(pe, z["pt_done"], b * G + (g + 1))
                wait(pe, z["v_done"], b + 1)
                for n in range(GH):
                    h = 8 * (n // 2) + 2 * g + n % 2
                    m = pe.matmul(PB[g % 2][:, n * (HD + 1):(n + 1) * (HD + 1)], PT[g % 2][:, n, :],
                                  vaug[par][:, h, :], start=True, stop=True)
                m.then_inc(z["pv_ready"], 1)

            def step(i, par, half):
                attn, proj, tail = within(i, 0), within(i, 1), within(i, -1)
                q, qh = 1 - par, (half + 1 if par else half)
                th = half if par else half - 1
                if attn:
                    scores(i)
                if tail:
                    t_o(i - 1)
                    t_wo(i - 1, i + 1 if attn else B)
                if proj:
                    p_xa(i + 1, q, qh)
                    p_h(i + 1, q)
                if tail:
                    t_x1T(i - 1, q)
                if proj:
                    wait(pe, z["h_done"], i + 2)
                    p_qk(i + 1, WqT, "q_ready")
                if tail:
                    t_w2(i - 1, q, th)
                if proj:
                    wait(pe, z["q_done"], i + 2)
                    p_qk(i + 1, WkT, "k_ready")
                if tail:
                    t_x2T(i - 1, q)
                if proj:
                    p_v(i + 1)
                if tail:
                    t_lg(i - 1)
                if attn:
                    transp(i, 0)
                if tail:
                    t_rank(i - 1, i + 2 if proj else B)
                if attn:
                    transp(i, 1)
                    pv(i, 0, par)
                    transp(i, 2)
                    pv(i, 1, par)
                    transp(i, 3)
                    pv(i, 2, par)
                    pv(i, 3, par)

            steps(pe, -1, B + 1, 3, B - 1, step)

            pe.wait_ge(z["selsum_done"], B + 1)
            pe.wait_ge(z["rank_done"], B)
            pe.matmul(M[1][:, 0:E], onesb[:], selsum[:], start=True, stop=True).then_inc(s_cnt, 1)

            pe.wait_ge(s_experts, 16 * 10)
            pe.wait_ge(s_plan, PLAN)

            def xt(t, par, half):
                wait(pe, s_gathered[par], (half + 1) * 16)
                wait(pe, f["xgT_done"], t - 1)
                for c in range(C):
                    m = pe.transpose(XTB[par][:, c * 128:(c + 1) * 128], xg[par][:, c * 128:(c + 1) * 128], ident[:])
                m.then_inc(f["xgT_ready"], 1)

            def gate_up(t, par):
                e = pe.value_load(tile_e[0:1, bass.ds(t, 1)], min_val=0, max_val=E - 1)
                wait(pe, f["xgT_done"], t + 1)
                wait(pe, f["gub_done"], t - 1)
                for c in range(C):
                    m = pe.matmul(GU[par][:], xgT[par][:, c * 128:(c + 1) * 128], Wgu[:, bass.ds(e * (C * 2 * D) + c * 2 * D, 2 * D)],
                                  start=(c == 0), stop=(c == C - 1))
                m.then_inc(f["gu_ready"], 1)

            def ht(t, par):
                wait(pe, f["hh_done"], t + 1)
                wait(pe, f["hhT_done"], t - 1)
                for c in range(C):
                    m = pe.transpose(HTB[par][:, c * 128:(c + 1) * 128], hh[par][:, c * 128:(c + 1) * 128], ident[:])
                m.then_inc(f["hhT_ready"], 1)

            def down(t, par):
                e = pe.value_load(tile_e[0:1, bass.ds(t, 1)], min_val=0, max_val=E - 1)
                wait(pe, f["hhT_done"], t + 1)
                wait(pe, f["yb_done"], t - 1)
                for c in range(C):
                    m = pe.matmul(YB[par][:, 0:H], hhT[par][:, c * 128:(c + 1) * 128], Wd[:, bass.ds(e * (C * H) + c * H, H)],
                                  start=(c == 0), stop=(c == C - 1))
                m.then_inc(f["y_ready"], 1)

            xt(0, 0, 0)

            def tstep(t, par, half):
                if within(t, -2, NT):
                    ht(t - 2, par)
                if within(t, 1, NT):
                    xt(t + 1, 1 - par, half + 1 if par else half)
                if within(t, 0, NT):
                    gate_up(t, par)
                if within(t, -2, NT):
                    down(t - 2, par)

            steps(pe, 0, NT + 2, 5, NT - 1, tstep)

        @block.scalar
        def _(act):
            act.wait_ge(s_const, 16 * len(CONSTS))

            def evac(dst, src, ready, done, b, free, free_count):
                wait(act, z[ready], b + 1)
                wait(act, z[free], free_count)
                act.activation(dst, src, ACT.Copy).then_inc(z[done], 1)

            def exps(b, g):
                wait(act, z["sub_done"], b * G + (g + 1))
                p = P[:, g].rearrange("q h t -> q (h t)")
                act.activation(p, p, ACT.Exp).then_inc(z["exp_done"], 1)

            def pt(b, g):
                wait(act, z["pt_ready"], b * G + (g + 1))
                wait(act, z["pv_ready"], b * G + (g - 1))
                act.activation(PT[g % 2][:].rearrange("q h t -> q (h t)"), PB[g % 2][:], ACT.Copy)\
                    .then_inc(z["pt_done"], 1)

            def two(t):
                return t[:].rearrange("p c t -> p (c t)")

            def step(i, par, half):
                attn, proj, tail = within(i, 0), within(i, 1), within(i, -1)
                if tail:
                    evac(two(oT), M[0][:, 0:C * S], "oT_ready", "oT_done", i - 1, "x1_ready", i - 1)
                if attn:
                    exps(i, 0)
                if proj:
                    evac(two(hT), M[1][:, 0:C * S], "h_ready", "h_done", i + 1, "v_ready", i + 1)
                if attn:
                    exps(i, 1)
                if tail:
                    evac(two(x1T), M[0][:, 0:C * S], "x1T_ready", "x1T_done", i - 1, "x2_ready", i - 1)
                if proj:
                    wait(act, z["q_ready"], i + 2)
                    wait(act, z["scores_ready"], (i + 1) * G)
                    for c in range(C):
                        m = act.activation(qT[:, c, :], M[1][:, c * S:(c + 1) * S], ACT.Identity, bias=bq[:, c:c + 1])
                    m.then_inc(z["q_done"], 1)
                if attn:
                    exps(i, 2)
                if tail:
                    evac(two(x2T), M[0][:, 0:C * S], "x2T_ready", "x2T_done", i - 1, "lg_ready", i - 1)
                if attn:
                    exps(i, 3)
                    pt(i, 0)
                if tail:
                    wait(act, z["dtop_done"], i)
                    act.activation(etop[:], dtop[:], ACT.Exp).then_inc(z["etop_done"], 1)
                if attn:
                    pt(i, 1)
                    pt(i, 2)
                    pt(i, 3)

            steps(act, -1, B + 1, 3, B - 1, step)

            def tstep(t, par, half):
                if within(t, -2, NT):
                    wait(act, f["hhT_ready"], t - 1)
                    wait(act, f["y_ready"], t - 3)
                    act.activation(hhT[par], HTB[par][:, 0:C * 128], ACT.Copy).then_inc(f["hhT_done"], 1)
                if within(t, 1, NT):
                    wait(act, f["xgT_ready"], t + 2)
                    wait(act, f["gu_ready"], t)
                    act.activation(xgT[1 - par], XTB[1 - par][:, 0:C * 128], ACT.Copy).then_inc(f["xgT_done"], 1)
                if within(t, -1, NT):
                    wait(act, f["gclip_done"], t)
                    act.activation(sg[1 - par][:], gu[1 - par][:, 0, :], ACT.Sigmoid, scale=ALPHA).then_inc(f["sig_done"], 1)
                if within(t, -3, NT):
                    wait(act, f["yb_done"], t - 2)
                    wait(act, f["ids_done"], t - 2)
                    wait(act, s_added, (t - 4) * 16)
                    act.activation(yw[1 - par][:], yb[1 - par][:], ACT.Copy, scale=ids[1 - par][:, 1:2].bitcast(F32))\
                        .then_inc(f["yw_done"], 1)

            tstep(-1, 1, -1)
            steps(act, 0, NT + 3, 5, NT - 1, tstep)

        @block.vector
        def _(dve):
            dve.memset(selsum[:], 0.0).then_inc(z["selsum_done"], 1)
            for i in range(2):
                last = dve.memset(vaug[i][:, :, HD:HD + 1], 1.0)
            dve.wait_ge(s_const, 16 * len(CONSTS))

            def heads(ap):
                return ap.rearrange("q (h d) -> q h d", h=NH)

            def softmax(b, g):
                wait(dve, z["scores_ready"], b * G + (g + 1))
                sc = SC[g][:].rearrange("q (h t) -> q h t", h=GH)
                dve.tensor_reduce(out=nmax[:, g], in_=sc, axis=AX.X, op=ALU.max, negate=True).then_inc(z["max_done"], 1)
                wait(dve, z["max_done"], b * G + (g + 1))
                wait(dve, z["pt_ready"], (b - 1) * G + (g + 1))
                dve.tensor_tensor(out=P[:, g], in0=sc, in1=nmax[:, g].unsqueeze(2).broadcast_to([S, GH, S]), op=ALU.add)\
                    .then_inc(z["sub_done"], 1)

            def norm(b, g):
                wait(dve, z["pv_ready"], b * G + (g + 1))
                pvo = PB[g % 2][:, 0:GH * (HD + 1)].rearrange("q (n d) -> q n d", d=HD + 1)
                dve.reciprocal(rsum[:, g % 2, :], pvo[:, :, HD]).then_inc(z["rsum_done"], 1)
                wait(dve, z["rsum_done"], b * G + (g + 1))
                wait(dve, z["oT_ready"], b)
                dve.tensor_tensor(out=group_heads(o[:], g),
                                  in0=pvo[:, :, 0:HD].rearrange("q (c p) d -> q c p d", c=C),
                                  in1=rsum[:, g % 2, :].rearrange("q (c p) -> q c p", c=C).unsqueeze(3)
                                  .broadcast_to([S, C, 2, HD]), op=ALU.mult).then_inc(z["norm_done"], 1)

            def x1_out(b, par, half):
                wait(dve, z["x1_ready"], b + 1)
                wait(dve, z["xb_done"], b + 1)
                wait(dve, s_x1_stored[par], half * 16)
                wait(dve, z["x1T_ready"], b - 1)
                dve.tensor_tensor(out=x1[par][:], in0=M[1][:, 0:H], in1=xb[:], op=ALU.add).then_inc(z["x1_done"], 1)

            def x2_out(b, par, half):
                wait(dve, z["x2_ready"], b + 1)
                wait(dve, s_x2_stored[par], half * 16)
                wait(dve, s_late[par], (half + 1) * 48)
                wait(dve, z["x2T_ready"], b - 1)
                dve.tensor_tensor(out=x2[par][:], in0=M[0][:, 0:H], in1=b2[par][:], op=ALU.add).then_inc(z["x2_done"], 1)

            def xa_out(b, par, half):
                wait(dve, z["xa_ready"], b + 1)
                wait(dve, s_early[par], (half + 1) * 64)
                wait(dve, z["h_ready"], b)
                dve.tensor_scalar(out=xa[:], in0=M[0][0:RANK, 0:S], scalar1=scal[par][:, 0:1], scalar2=None, op0=ALU.mult)\
                    .then_inc(z["xa_done"], 1)

            def k_out(b):
                wait(dve, z["k_ready"], b + 1)
                wait(dve, z["scores_ready"], b * G)
                for e in range(2):
                    for c in range(C):
                        m = dve.tensor_scalar(out=kM[:, c, e, :], in0=M[1][:, c * S:(c + 1) * S], scalar1=bk[:, c:c + 1],
                                              scalar2=kmask[:, e:e + 1], op0=ALU.add, op1=ALU.mult)
                    m.then_inc(z["k_done"], 1)

            def v_out(b, par):
                wait(dve, z["v_ready"], b + 1)
                wait(dve, z["pv_ready"], (b - 1) * G)
                dve.tensor_tensor(out=vaug[par][:, :, 0:HD], in0=heads(M[1][:, 0:H]), in1=heads(bv[:]), op=ALU.add)\
                    .then_inc(z["v_done"], 1)

            def choose(b):
                wait(dve, z["lg_ready"], b + 1)
                dve.tensor_tensor(out=lg[:], in0=M[0][:, 0:E], in1=rbias[:], op=ALU.add).then_inc(z["lg_done"], 1)
                stand_alone(dve, (z["lg_done"], b + 1), (z["etop_done"], b))
                dve.max(out=top8[:], in_=lg[:]).then_inc(z["top_done"], 1)
                stand_alone(dve, (z["top_done"], b + 1))
                dve.max_index(out=topi[:], in_max=top8[:], in_values=lg[:]).then_inc(z["topi_done"], 1)
                dve.tensor_scalar(out=dtop[:], in0=top8[:, 0:TOPK], scalar1=top8[:, 0:1], scalar2=None, op0=ALU.subtract)\
                    .then_inc(z["dtop_done"], 1)
                wait(dve, z["topi_done"], b + 1)
                dve.tensor_copy(topf[:], topi[:, 0:TOPK]).then_inc(z["topf_done"], 1)
                wait(dve, z["topf_done"], b + 1)
                dve.tensor_tensor(out=onehot[:], in0=topf[:].unsqueeze(2).broadcast_to([S, TOPK, E]),
                                  in1=iota_e[:].unsqueeze(1).broadcast_to([S, TOPK, E]), op=ALU.is_equal)\
                    .then_inc(z["onehot_done"], 1)
                wait(dve, z["onehot_done"], b + 1)
                wait(dve, z["rank_ready"], b)
                with nc.allow_low_precision(reason="ones and zeros"):
                    dve.tensor_reduce(out=sel[:], in_=onehot[:].rearrange("p j e -> p e j"), axis=AX.X, op=ALU.add)\
                        .then_inc(z["sel_done"], 1)

            def place(b, par, half):
                wait(dve, z["rank_ready"], b + 1)
                dve.tensor_tensor(out=rank[:], in0=M[1][:, 0:E], in1=ebase[:], op=ALU.add).then_inc(z["rank_done"], 1)
                dve.tensor_tensor(out=selsum[:], in0=selsum[:], in1=sel[:], op=ALU.add).then_inc(z["selsum_done"], 1)
                wait(dve, z["rank_done"], b + 1)
                dve.tensor_tensor(out=prod[:], in0=onehot[:], in1=rank[:].unsqueeze(1).broadcast_to([S, TOPK, E]),
                                  op=ALU.mult).then_inc(z["prod_done"], 1)
                wait(dve, z["etop_done"], b + 1)
                dve.tensor_reduce(out=esum[:], in_=etop[:], axis=AX.X, op=ALU.add).then_inc(z["esum_done"], 1)
                wait(dve, z["prod_done"], b + 1)
                with nc.allow_low_precision(reason="whole numbers below 2^24"):
                    dve.tensor_reduce(out=slot[:], in_=prod[:], axis=AX.X, op=ALU.add).then_inc(z["slot_done"], 1)
                wait(dve, z["esum_done"], b + 1)
                dve.reciprocal(einv[:], esum[:]).then_inc(z["einv_done"], 1)
                wait(dve, z["slot_done"], b + 1)
                dve.tensor_scalar(out=slot_p[:], in0=slot[:], scalar1=127, scalar2=None, op0=ALU.bitwise_and)\
                    .then_inc(z["slotp_done"], 1)
                dve.tensor_scalar(out=slot_c[:], in0=slot[:], scalar1=7, scalar2=None, op0=ALU.arith_shift_right)\
                    .then_inc(z["slotc_done"], 1)
                wait(dve, s_scattered[par], half * (16 * TOPK))
                wait(dve, z["einv_done"], b + 1)
                dve.tensor_scalar(out=pair[par][:, :, 1].bitcast(F32), in0=etop[:], scalar1=einv[:, 0:1], scalar2=None,
                                  op0=ALU.mult)
                dve.tensor_scalar(out=pair[par][:, :, 0], in0=pair[par][:, :, 0], scalar1=float(2 * S), scalar2=None,
                                  op0=ALU.add).then_inc(z["pair_done"], 1)
                wait(dve, z["slotp_done"], b + 1)
                wait(dve, z["slotc_done"], b + 1)
                dve.scalar_tensor_tensor(out=slot_row[par][:], in0=slot_p[:], scalar=float(TCOLS), in1=slot_c[:],
                                         op0=ALU.mult, op1=ALU.add).then_inc(z["slotrow_done"], 1)

            def step(i, par, half):
                attn, proj, tail = within(i, 0), within(i, 1), within(i, -1)
                q, qh = 1 - par, (half + 1 if par else half)
                th = half if par else half - 1
                if attn:
                    softmax(i, 0)
                if tail:
                    x1_out(i - 1, q, th)
                if proj:
                    xa_out(i + 1, q, qh)
                if attn:
                    softmax(i, 1)
                if tail:
                    x2_out(i - 1, q, th)
                if attn:
                    softmax(i, 2)
                if proj:
                    k_out(i + 1)
                if attn:
                    softmax(i, 3)
                if proj:
                    v_out(i + 1, q)
                if tail:
                    choose(i - 1)
                    place(i - 1, q, th)
                if attn:
                    for g in range(G):
                        norm(i, g)

            steps(dve, -1, B + 1, 3, B - 1, step)

            dve.wait_ge(s_cnt, 1)
            n = [0]

            def then(m):
                m.then_inc(s_plan, 1)
                n[0] += 1
                dve.wait_ge(s_plan, n[0])

            def tiles_of(ap):
                return ap.unsqueeze(1).broadcast_to([1, NT, E])

            then(dve.memset(one_e[:], 1.0))
            then(dve.tensor_scalar(out=cnt[:], in0=M[1][0:1, 0:E], scalar1=127.0, scalar2=None, op0=ALU.add))
            then(dve.tensor_scalar(out=ntile[:], in0=cnt[:], scalar1=7, scalar2=None, op0=ALU.arith_shift_right))
            then(dve.tensor_copy(ntilef[:], ntile[:]))
            then(dve.tensor_tensor_scan(out=cum[:], data0=one_e[:], data1=ntilef[:], initial=0.0, op0=ALU.mult, op1=ALU.add))
            then(dve.tensor_tensor(out=past, in0=iota_t[:].unsqueeze(2).broadcast_to([1, NT, E]), in1=tiles_of(cum[:]),
                                   op=ALU.is_ge))
            then(dve.tensor_reduce(out=t_e[:], in_=past, axis=AX.X, op=ALU.add))
            then(dve.tensor_tensor(out=past, in0=past, in1=tiles_of(ntilef[:]), op=ALU.mult))
            then(dve.tensor_reduce(out=t_s[:], in_=past, axis=AX.X, op=ALU.add))
            then(dve.scalar_tensor_tensor(out=t_r[:], in0=t_e[:], scalar=float(RT), in1=iota_t[:], op0=ALU.mult, op1=ALU.add))
            then(dve.tensor_tensor(out=t_r[:], in0=t_r[:], in1=t_s[:], op=ALU.subtract))
            then(dve.tensor_scalar(out=tile_c[:], in0=t_r[:], scalar1=float(TCOLS - 1), scalar2=None, op0=ALU.min))
            then(dve.tensor_scalar(out=tile_e[:], in0=t_e[:], scalar1=float(E - 1), scalar2=None, op0=ALU.min))
            assert n[0] == PLAN

            dve.wait_ge(s_experts, 16 * 10)

            def tstep(t, par, half):
                q = 1 - par
                if within(t, -1, NT):
                    e = dve.value_load(tile_e[0:1, bass.ds(t - 1, 1)], min_val=0, max_val=E - 1)
                    wait(dve, f["gu_ready"], t)
                    g2 = gu[q][:].rearrange("p k d -> p (k d)")
                    dve.tensor_tensor(out=g2, in0=GU[q][:], in1=bgu[:, bass.ds(e * (2 * D), 2 * D)], op=ALU.add)\
                        .then_inc(f["gub_done"], 1)
                    wait(dve, f["gub_done"], t)
                    dve.tensor_scalar(out=gu[q][:, 0, :], in0=gu[q][:, 0, :], scalar1=LIMIT, scalar2=None, op0=ALU.min)\
                        .then_inc(f["gclip_done"], 1)
                    dve.tensor_scalar(out=gu[q][:, 1, :], in0=gu[q][:, 1, :], scalar1=LIMIT, scalar2=-LIMIT,
                                      op0=ALU.min, op1=ALU.max).then_inc(f["uclip_done"], 1)
                if within(t, -3, NT):
                    e = dve.value_load(tile_e[0:1, bass.ds(t - 3, 1)], min_val=0, max_val=E - 1)
                    wait(dve, f["y_ready"], t - 2)
                    wait(dve, f["yw_done"], t - 4)
                    dve.tensor_tensor(out=yb[q][:], in0=YB[q][:, 0:H], in1=bd[:, bass.ds(e * H, H)], op=ALU.add)\
                        .then_inc(f["yb_done"], 1)
                if within(t, -1, NT):
                    wait(dve, f["sig_done"], t)
                    dve.tensor_tensor(out=sg[q][:], in0=sg[q][:], in1=gu[q][:, 0, :], op=ALU.mult).then_inc(f["glu_done"], 1)
                    wait(dve, f["glu_done"], t)
                    wait(dve, f["uclip_done"], t)
                    wait(dve, f["hhT_ready"], t - 2)
                    dve.scalar_tensor_tensor(out=hh[q][:], in0=gu[q][:, 1, :], scalar=1.0, in1=sg[q][:],
                                             op0=ALU.add, op1=ALU.mult).then_inc(f["hh_done"], 1)

            steps(dve, 0, NT + 3, 5, NT - 1, tstep)


PLAN = 13


def kernel(**inputs):
    import numpy as np
    import ml_dtypes
    import concourse.bacc as bacc
    from concourse.bass_utils import run_bass_kernel_spmd

    v = {k: np.asarray(x) for k, x in inputs.items()}
    bf = ml_dtypes.bfloat16

    def chunked(w):
        return w.reshape(-1, 128, w.shape[-1]).transpose(1, 0, 2)

    def apart(w):
        return np.concatenate([w[..., ::2], w[..., 1::2]], -1)

    p = np.arange(128)
    q, k = p[:, None], p[None, :]
    mask = np.where(k <= q, 0.0, -2.0 ** 100)
    table = np.zeros((128, TCOLS, 2), np.int32)
    table[:, :, 0] = ROWS + q
    pair = np.zeros((2, 128, TOPK, 2), np.int32)
    pair[:, :, :, 0] = (p[:, None] + 128 * np.arange(2)[:, None, None] - 2 * S)
    even = (p // HD) % 2 == 0
    arrays = {
        "idx": np.concatenate([v["itok_B_0_6"], v["itok_B_0_15"]]).reshape(1, 2 * B),
        "xT": v["x"].reshape(B, S, C, 128).transpose(0, 3, 2, 1),
        "x": v["x"],
        "AT": v["L0_cond_A"].reshape(8, RANK, C, 128).transpose(0, 3, 2, 1),
        "BT": v["L0_cond_Bm"].transpose(0, 2, 1),
        "scal": v["L0_cond_scalings"],
        "W2": v["L0_cond2_W"].reshape(E, C, 128, H).transpose(0, 2, 1, 3),
        "b2": v["L0_cond2_b"],
        "WT": chunked(v["L0_cond_W"].T),
        "WqT": chunked(v["L0_attn_Wq"].T),
        "WkT": chunked(v["L0_attn_Wk"].T),
        "WvT": chunked(v["L0_attn_Wv"].T),
        "WoT": chunked(v["L0_attn_Wo"].T),
        "RWT": chunked(v["L0_ffn_router_weight"].T),
        "bq": v["L0_attn_bq"].reshape(C, 128).T,
        "bk": v["L0_attn_bk"].reshape(C, 128).T,
        "bv": v["L0_attn_bv"],
        "bo": v["L0_attn_bo"],
        "rbias": v["L0_ffn_router_bias"],
        "Wgu": apart(v["L0_ffn_gate_up_proj"]).reshape(E, C, 128, 2 * D).transpose(2, 0, 1, 3).reshape(128, -1),
        "Wd": v["L0_ffn_down_proj"].reshape(E, C, 128, H).transpose(2, 0, 1, 3).reshape(128, -1),
        "bgu": apart(v["L0_ffn_gate_up_proj_bias"]).reshape(-1),
        "bd": v["L0_ffn_down_proj_bias"].reshape(-1),
        "ident": np.eye(128, dtype=np.float32),
        "identb": np.eye(128).astype(bf),
        "causal": np.tile(mask, (1, GH)).astype(bf),
        "tri": (q < k).astype(bf),
        "onesb": np.ones((128, 128), bf),
        "iota_e": np.tile(np.arange(E, dtype=np.float32), (128, 1)),
        "ebase": np.tile(np.arange(E, dtype=np.float32) * ROWS, (128, 1)),
        "iota_t": np.arange(NT, dtype=np.float32).reshape(1, NT),
        "kmask": np.stack([even, ~even], 1).astype(np.float32) / np.float32(HD ** 0.5),
        "table": table.reshape(128, -1),
        "pair0": pair[0],
        "pair1": pair[1],
    }
    nc = bacc.Bacc("TRN2", target_bir_lowering=False, num_devices=1)
    feeds, aps = {}, {}
    for name, arr in arrays.items():
        arr = np.ascontiguousarray(arr)
        feeds[f"in_{name}"] = arr
        aps[name] = nc.dram_tensor(f"in_{name}", arr.shape, mybir.dt.from_np(arr.dtype), kind="ExternalInput").ap()
    out = nc.dram_tensor("out_rows", (ROWS + PADROWS, H), F32, kind="ExternalOutput").ap()
    adaln_attn_moe(nc, aps, out)
    r = run_bass_kernel_spmd(nc, [feeds], core_ids=[0])
    return r.results[0]["out_rows"][:ROWS].reshape(B, S, H)
```

```python
import concourse.bass as bass
from concourse import mybir
from contextlib import ExitStack

F32 = mybir.dt.float32
BF16 = mybir.dt.bfloat16
I32 = mybir.dt.int32
U32 = mybir.dt.uint32
ALU = mybir.AluOpType
ACT = mybir.ActivationFunctionType
AX = mybir.AxisListType

B = 16
S = 128
H = 256
C = H // 128
NH = 16
HD = H // NH
G = 4
GH = NH // G
RANK = 16
E = 16
D = 256
TOPK = 4
ALPHA = 1.702
LIMIT = 7.0
ROWS = B * S
NT = ROWS * TOPK // 128 + E - 1
RT = ROWS // 128
TCOLS = E * RT + 1
PADROWS = 128


def adaln_attn_moe(nc: bass.Bass, a, out):
    ctx = ExitStack()
    with ctx:
        def sb(name, shape, dt=F32):
            return ctx.enter_context(nc.sbuf_tensor(name, shape, dt))

        def ps(name, dt=F32):
            return ctx.enter_context(nc.psum_tensor(name, [128, 512], dt))

        def sem(name):
            return ctx.enter_context(nc.semaphore(name))

        x2_rows = nc.dram_tensor("x2_rows", [ROWS + PADROWS, H], F32, kind="Internal").ap()
        slot_table = nc.dram_tensor("slot_table", [128 * TCOLS, 2], I32, kind="Internal").ap()
        table_by_row = slot_table.rearrange("(p c) two -> p (c two)", c=TCOLS)

        ident = sb("ident", [128, 128])
        identb = sb("identb", [128, 128], BF16)
        causal = sb("causal", [128, GH * 128], BF16)
        tri = sb("tri", [128, 128], BF16)
        onesb = sb("onesb", [128, 128], BF16)
        iota_e = sb("iota_e", [128, E])
        ebase = sb("ebase", [128, E])
        iota_t = sb("iota_t", [1, NT])
        kmask = sb("kmask", [128, GH])
        idx = sb("idx", [1, 2 * B], I32)
        WT = sb("WT", [128, C, H])
        WqT = sb("WqT", [128, C, H])
        WkT = sb("WkT", [128, C, H])
        WvT = sb("WvT", [128, C, H])
        WoT = sb("WoT", [128, C, H])
        RWT = sb("RWT", [128, C, E])
        bq = sb("bq", [128, C])
        bk = sb("bk", [128, C])
        bv = sb("bv", [128, H])
        bo = sb("bo", [128, H])
        rbias = sb("rbias", [128, E])

        xT = [sb(f"xT{i}", [128, C, S]) for i in range(2)]
        AT = [sb(f"AT{i}", [128, C, RANK]) for i in range(2)]
        BT = [sb(f"BT{i}", [RANK, H]) for i in range(2)]
        scal = [sb(f"scal{i}", [RANK, 1]) for i in range(2)]
        xrow = [sb(f"xrow{i}", [S, H]) for i in range(2)]
        W2 = [sb(f"W2_{i}", [128, C, H]) for i in range(2)]
        b2 = [sb(f"b2_{i}", [S, H]) for i in range(2)]
        xa = sb("xa", [RANK, S])
        hT = sb("hT", [128, C, S])
        qT = sb("qT", [128, C, S])
        kT = sb("kT", [128, C, S])
        kM = sb("kM", [128, C, GH, S])
        vaug = [sb(f"vaug{i}", [S, NH, HD + 1]) for i in range(2)]
        P = sb("P", [S, G, GH, S])
        nmax = sb("nmax", [S, G, GH])
        PT = [sb(f"PT{i}", [S, GH, S]) for i in range(2)]
        rsum = sb("rsum", [S, 2, GH])
        o = sb("o", [S, NH, HD])
        oT = sb("oT", [128, C, S])
        xb = sb("xb", [S, H])
        x1 = [sb(f"x1_{i}", [S, H]) for i in range(2)]
        x1T = sb("x1T", [128, C, S])
        x2 = [sb(f"x2_{i}", [S, H]) for i in range(2)]
        x2T = sb("x2T", [128, C, S])
        lg = sb("lg", [S, E])
        top8 = sb("top8", [S, 8])
        topi = sb("topi", [S, 8], U32)
        topf = sb("topf", [S, TOPK])
        onehot = sb("onehot", [S, TOPK, E])
        sel = sb("sel", [S, E], BF16)
        selsum = sb("selsum", [S, E], BF16)
        rank = sb("rank", [S, E])
        prod = sb("prod", [S, TOPK, E])
        slot = sb("slot", [S, TOPK], I32)
        slot_p = sb("slot_p", [S, TOPK], I32)
        slot_c = sb("slot_c", [S, TOPK], I32)
        slot_row = [sb(f"slot_row{i}", [S, TOPK], I32) for i in range(2)]
        pair = [sb(f"pair{i}", [S, TOPK, 2], I32) for i in range(2)]
        dtop = sb("dtop", [S, TOPK])
        etop = sb("etop", [S, TOPK])
        esum = sb("esum", [S, 1])
        einv = sb("einv", [S, 1])

        Wgu = sb("Wgu", [128, E * C * 2 * D])
        Wd = sb("Wd", [128, E * C * H])
        bgu = sb("bgu", [128, E * 2 * D])
        bd = sb("bd", [128, E * H])
        table = kM[:].rearrange("p c h t -> p (c h t)")[:, 0:TCOLS * 2].bitcast(I32)
        zrow = sb("zrow", [128, H])

        cnt = sb("cnt", [1, E], I32)
        ntile = sb("ntile", [1, E], I32)
        ntilef = sb("ntilef", [1, E])
        cum = sb("cum", [1, E])
        one_e = sb("one_e", [1, E])
        past = P[0:1].rearrange("p g h s -> p (g h s)")[:, 0:NT * E].rearrange("p (t e) -> p t e", e=E)
        t_e = sb("t_e", [1, NT])
        t_s = sb("t_s", [1, NT])
        t_r = sb("t_r", [1, NT])
        tile_e = sb("tile_e", [1, NT], I32)
        tile_c = sb("tile_c", [1, NT], I32)

        idg = [sb(f"idg{i}", [128, 2], I32) for i in range(2)]
        ids = [sb(f"ids{i}", [128, 2], I32) for i in range(2)]
        def halves(t):
            w = t[:].rearrange("p c n -> p (c n)")
            return [w[:, 0:H], w[:, H:2 * H]]

        xg = halves(WvT)
        xgT = halves(PT[0])
        gu = [P[:, 2 + i].rearrange("p h s -> p (h s)").rearrange("p (k d) -> p k d", k=2) for i in range(2)]
        hhT = halves(PT[1])
        hh = halves(W2[0])
        sg = halves(W2[1])
        yb = halves(WqT)
        yw = halves(WkT)

        bank = [ps(f"bank{i}") for i in range(8)]
        SC = bank[0:4]
        PB = bank[4:6]
        M = bank[6:8]
        GU = bank[0:2]
        XTB = bank[2:4]
        HTB = bank[4:6]
        YB = bank[6:8]

        s_const = sem("const_loaded")
        s_idx = sem("idx_loaded")
        s_early = [sem(f"early_loaded{i}") for i in range(2)]
        s_late = [sem(f"late_loaded{i}") for i in range(2)]
        s_experts = sem("experts_loaded")
        s_init = sem("init_done")
        s_tinit = sem("table_init_stored")
        names = ("xa_ready xa_done h_ready h_done q_ready q_done k_ready k_done v_ready v_done scores_ready "
                 "km_done max_done sub_done exp_done pt_ready pt_done pv_ready rsum_done norm_done oT_ready oT_done "
                 "x1_ready x1_done x1T_ready x1T_done x2_ready x2_done x2T_ready x2T_done lg_ready lg_done "
                 "xb_done top_done topi_done topf_done onehot_done sel_done rank_ready rank_done prod_done "
                 "slot_done slotp_done slotc_done slotrow_done dtop_done etop_done esum_done einv_done "
                 "pair_done selsum_done").split()
        z = {n: sem(n) for n in names}
        s_x1_stored = [sem(f"x1_stored{i}") for i in range(2)]
        s_x2_stored = [sem(f"x2_stored{i}") for i in range(2)]
        s_scattered = [sem(f"pairs_scattered{i}") for i in range(2)]
        s_pad = sem("pad_rows_stored")
        s_passed = sem("waits_passed")
        s_cnt = sem("counts_ready")
        s_plan = sem("plan_steps")
        s_table = sem("table_loaded")
        s_gathered = [sem(f"rows_gathered{i}") for i in range(2)]
        s_added = sem("rows_added")
        names = ("idg_done ids_done xgT_ready xgT_done gu_ready gub_done gclip_done uclip_done sig_done glu_done "
                 "hh_done hhT_ready hhT_done y_ready yb_done yw_done").split()
        f = {n: sem(n) for n in names}

        def wait(eng, s, value):
            if not isinstance(value, int) or value > 0:
                eng.wait_ge(s, value)

        def stand_alone(eng, *waits):
            for s, v in waits:
                wait(eng, s, v)
            eng.sem_inc(s_passed, 1)

        def steps(eng, lo, hi, full_lo, full_hi, body):
            for t in range(lo, full_lo):
                body(t, t % 2, t // 2)
            with eng.Fori(0, (full_hi - full_lo) // 2) as j:
                for u in range(2):
                    body(j * 2 + (full_lo + u), (full_lo + u) % 2, j + (full_lo + u) // 2)
            for t in range(full_hi, hi):
                body(t, t % 2, t // 2)

        def within(t, off, n=B):
            return not isinstance(t, int) or 0 <= t + off < n

        block = ctx.enter_context(nc.Block())

        CONSTS = ((ident, "ident"), (identb, "identb"), (causal, "causal"), (tri, "tri"), (onesb, "onesb"),
                  (iota_e, "iota_e"), (ebase, "ebase"), (iota_t, "iota_t"), (kmask, "kmask"), (WT, "WT"), (WqT, "WqT"),
                  (WkT, "WkT"), (WvT, "WvT"), (WoT, "WoT"), (RWT, "RWT"), (bq, "bq"), (bk, "bk"), (bv, "bv"),
                  (bo, "bo"), (rbias, "rbias"), (pair[0], "pair0"), (pair[1], "pair1"))

        @block.sync
        def _(sp):
            sp.dma_start(idx[:, :], a["idx"]).then_inc(s_idx, 16)
            for dst, name in CONSTS:
                src = a[name].partition_broadcast(128) if name in ("bv", "bo", "rbias") else a[name]
                sp.dma_start(dst[:], src).then_inc(s_const, 16)
            sp.wait_ge(s_idx, 16)

            def early(b, par, half):
                wait(sp, z["h_ready"], b - 1)
                ad = sp.value_load(idx[0:1, bass.ds(b, 1)], min_val=0, max_val=7)
                sp.dma_start(xT[par][:], a["xT"][bass.ds(b, 1)].rearrange("o p c t -> (o p) c t")).then_inc(s_early[par], 16)
                sp.dma_start(AT[par][:], a["AT"][bass.ds(ad, 1)].rearrange("o p c r -> (o p) c r")).then_inc(s_early[par], 16)
                sp.dma_start(BT[par][:], a["BT"][bass.ds(ad, 1)].rearrange("o r h -> (o r) h")).then_inc(s_early[par], 16)
                sp.dma_start(scal[par][:], a["scal"][bass.ds(ad, 1)].partition_broadcast(RANK)).then_inc(s_early[par], 16)

            def late(b, par, half):
                wait(sp, z["x2_done"], b - 1)
                wait(sp, z["xb_done"], b - 1)
                ex = sp.value_load(idx[0:1, bass.ds(b + B, 1)], min_val=0, max_val=E - 1)
                sp.dma_start(xrow[par][:], a["x"][bass.ds(b, 1)].rearrange("o t h -> (o t) h")).then_inc(s_late[par], 16)
                sp.dma_start(W2[par][:], a["W2"][bass.ds(ex, 1)].rearrange("o p c h -> (o p) c h")).then_inc(s_late[par], 16)
                sp.dma_start(b2[par][:], a["b2"][bass.ds(ex, 1)].rearrange("o h -> (o h)").partition_broadcast(S)).then_inc(s_late[par], 16)

            def store(b, par, half):
                wait(sp, z["x1_done"], b + 1)
                sp.dma_start(out[bass.ds(b * S, S)], x1[par][:]).then_inc(s_x1_stored[par], 16)
                wait(sp, z["x2_done"], b + 1)
                sp.dma_start(x2_rows[bass.ds(b * S, S)], x2[par][:]).then_inc(s_x2_stored[par], 16)

            early(0, 0, 0)
            early(1, 1, 0)
            late(0, 0, 0)
            sp.dma_start(table_by_row, a["table"]).then_inc(s_tinit, 16)
            sp.wait_ge(s_init, 1)
            sp.dma_start(x2_rows[ROWS:ROWS + PADROWS], zrow[:]).then_inc(s_pad, 16)
            sp.dma_start(out[ROWS:ROWS + PADROWS], zrow[:]).then_inc(s_pad, 16)

            def step(i, par, half):
                if within(i, 2):
                    early(i + 2, par, half + 1)
                if within(i, -1):
                    store(i - 1, 1 - par, half if par else half - 1)
                if within(i, 1):
                    late(i + 1, 1 - par, half + 1 if par else half)
                if isinstance(i, int) and i == 0:
                    for e in range(0, E, 4):
                        sp.dma_start(Wgu[:, e * C * 2 * D:(e + 4) * C * 2 * D],
                                     a["Wgu"][:, e * C * 2 * D:(e + 4) * C * 2 * D]).then_inc(s_experts, 16)
                        sp.dma_start(Wd[:, e * C * H:(e + 4) * C * H],
                                     a["Wd"][:, e * C * H:(e + 4) * C * H]).then_inc(s_experts, 16)
                    sp.dma_start(bgu[:], a["bgu"].partition_broadcast(128)).then_inc(s_experts, 16)
                    sp.dma_start(bd[:], a["bd"].partition_broadcast(128)).then_inc(s_experts, 16)

            steps(sp, 0, B + 1, 1, 13, step)

            for par in range(2):
                sp.wait_ge(s_scattered[par], 16 * TOPK * (B // 2))
            sp.dma_start(table[:, :], table_by_row).then_inc(s_table, 16)
            sp.wait_ge(s_added, 16 * NT)

        @block.gpsimd
        def _(pool):
            pool.memset(zrow[:], 0.0).then_inc(s_init, 1)
            pool.wait_ge(s_const, 16 * len(CONSTS))

            def residual(b, par, half):
                wait(pool, s_late[par], (half + 1) * 48)
                wait(pool, z["x1_done"], b)
                pool.tensor_tensor(out=xb[:], in0=xrow[par][:], in1=bo[:], op=ALU.add).then_inc(z["xb_done"], 1)

            def mask_k(b):
                wait(pool, z["k_done"], b + 1)
                wait(pool, z["scores_ready"], b * G)
                for c in range(C):
                    m = pool.tensor_tensor(out=kM[:, c], in0=kT[:, c, :].unsqueeze(1).broadcast_to([128, GH, S]),
                                           in1=kmask[:].unsqueeze(2).broadcast_to([128, GH, S]), op=ALU.mult)
                m.then_inc(z["km_done"], 1)

            def scatter(b, bp):
                stand_alone(pool, (z["slotrow_done"], b + 1), (z["pair_done"], b + 1))
                if isinstance(b, int) and b == 0:
                    pool.wait_ge(s_tinit, 16)
                for j in range(TOPK):
                    pool.indirect_dma_start(
                        out=slot_table, out_offset=bass.IndirectOffsetOnAxis(ap=slot_row[bp][:, j:j + 1], axis=0),
                        in_=pair[bp][:, j, :], in_offset=None).then_inc(s_scattered[bp], 16)

            def step(i, par, half):
                if within(i, -1):
                    residual(i - 1, 1 - par, half if par else half - 1)
                if within(i, -2):
                    scatter(i - 2, par)
                if within(i, 1):
                    mask_k(i + 1)

            steps(pool, -1, B + 2, 3, B - 1, step)

            pool.wait_ge(s_table, 16)
            pool.wait_ge(s_plan, PLAN)
            for par in range(2):
                pool.wait_ge(s_x2_stored[par], 16 * (B // 2))
                pool.wait_ge(s_x1_stored[par], 16 * (B // 2))
            pool.wait_ge(s_pad, 32)

            def gather(t, par, half):
                c = pool.value_load(tile_c[0:1, bass.ds(t, 1)], min_val=0, max_val=TCOLS - 1)
                wait(pool, s_gathered[par], half * 16)
                pool.tensor_copy(idg[par][:], table[:, bass.ds(c * 2, 2)]).then_inc(f["idg_done"], 1)
                stand_alone(pool, (f["idg_done"], t + 1), (f["xgT_ready"], t - 1))
                pool.indirect_dma_start(
                    out=xg[par][:], out_offset=None, in_=x2_rows,
                    in_offset=bass.IndirectOffsetOnAxis(ap=idg[par][:, 0:1], axis=0)).then_inc(s_gathered[par], 16)

            def add(t, par):
                stand_alone(pool, (f["yw_done"], t + 1), (s_added, t * 16))
                pool.indirect_dma_start(
                    out=out, out_offset=bass.IndirectOffsetOnAxis(ap=ids[par][:, 0:1], axis=0),
                    in_=yw[par][:], in_offset=None, compute_op=ALU.add).then_inc(s_added, 16)

            def keep(t, par):
                c = pool.value_load(tile_c[0:1, bass.ds(t, 1)], min_val=0, max_val=TCOLS - 1)
                wait(pool, s_added, (t - 1) * 16)
                pool.tensor_copy(ids[par][:], table[:, bass.ds(c * 2, 2)]).then_inc(f["ids_done"], 1)

            for t in range(3):
                gather(t, t % 2, t // 2)

            def tstep(t, par, half):
                if within(t, -3, NT):
                    add(t - 3, 1 - par)
                if within(t, -2, NT):
                    keep(t - 2, par)
                if within(t, 3, NT):
                    gather(t + 3, 1 - par, half + 2 if par else half + 1)

            steps(pool, 0, NT + 3, 6, NT - 3, tstep)

        @block.tensor
        def _(pe):
            pe.wait_ge(s_const, 16 * len(CONSTS))

            def t_o(b):
                wait(pe, z["norm_done"], b * G + G)
                wait(pe, z["lg_done"], b)
                of = o[:].rearrange("q h d -> q (h d)")
                for c in range(C):
                    m = pe.transpose(M[0][:, c * S:(c + 1) * S], of[:, c * 128:(c + 1) * 128], ident[:])
                m.then_inc(z["oT_ready"], 1)

            def t_wo(b):
                wait(pe, z["oT_done"], b + 1)
                wait(pe, z["rank_done"], b)
                wait(pe, z["v_done"], b + 2 if within(b, 1) else B)
                for c in range(C):
                    m = pe.matmul(M[1][:, 0:H], oT[:, c, :], WoT[:, c, :], start=(c == 0), stop=(c == C - 1))
                m.then_inc(z["x1_ready"], 1)

            def t_x1T(b, par):
                wait(pe, z["x1_done"], b + 1)
                wait(pe, z["xa_done"], b + 1)
                for c in range(C):
                    m = pe.transpose(M[0][:, c * S:(c + 1) * S], x1[par][:, c * 128:(c + 1) * 128], ident[:])
                m.then_inc(z["x1T_ready"], 1)

            def t_w2(b, par, half):
                wait(pe, s_late[par], (half + 1) * 48)
                wait(pe, z["x1T_done"], b + 1)
                for c in range(C):
                    m = pe.matmul(M[0][:, 0:H], x1T[:, c, :], W2[par][:, c, :], start=(c == 0), stop=(c == C - 1))
                m.then_inc(z["x2_ready"], 1)

            def t_x2T(b, par):
                wait(pe, z["x2_done"], b + 1)
                for c in range(C):
                    m = pe.transpose(M[0][:, c * S:(c + 1) * S], x2[par][:, c * 128:(c + 1) * 128], ident[:])
                m.then_inc(z["x2T_ready"], 1)

            def t_lg(b):
                wait(pe, z["x2T_done"], b + 1)
                for c in range(C):
                    m = pe.matmul(M[0][:, 0:E], x2T[:, c, :], RWT[:, c, :], start=(c == 0), stop=(c == C - 1))
                m.then_inc(z["lg_ready"], 1)

            def t_rank(b):
                wait(pe, z["sel_done"], b + 1)
                wait(pe, z["selsum_done"], b + 1)
                wait(pe, z["v_done"], b + 3 if within(b, 2) else B)
                pe.matmul(M[1][:, 0:E], tri[:], sel[:], start=True, stop=False)
                pe.matmul(M[1][:, 0:E], onesb[:], selsum[:], start=False, stop=True).then_inc(z["rank_ready"], 1)

            def p_xa(b, par, half):
                wait(pe, s_early[par], (half + 1) * 64)
                wait(pe, z["oT_done"], b - 1)
                wait(pe, z["lg_done"], b - 2)
                for c in range(C):
                    m = pe.matmul(M[0][0:RANK, 0:S], AT[par][:, c, :], xT[par][:, c, :], start=(c == 0), stop=(c == C - 1))
                m.then_inc(z["xa_ready"], 1)

            def p_h(b, par):
                wait(pe, z["xa_done"], b + 1)
                wait(pe, z["x1_done"], b - 1)
                wait(pe, z["v_done"], b)
                for k in range(C):
                    dst = M[1][:, k * S:(k + 1) * S]
                    for c in range(C):
                        pe.matmul(dst, WT[:, c, k * 128:(k + 1) * 128], xT[par][:, c, :], start=(c == 0), stop=False)
                    m = pe.matmul(dst, BT[par][:, k * 128:(k + 1) * 128], xa[:], start=False, stop=True)
                m.then_inc(z["h_ready"], 1)

            def p_qk(b, w, ready):
                for k in range(C):
                    for c in range(C):
                        m = pe.matmul(M[1][:, k * S:(k + 1) * S], w[:, c, k * 128:(k + 1) * 128], hT[:, c, :],
                                      start=(c == 0), stop=(c == C - 1))
                m.then_inc(z[ready], 1)

            def p_v(b):
                wait(pe, z["k_done"], b + 1)
                for c in range(C):
                    m = pe.matmul(M[1][:, 0:H], hT[:, c, :], WvT[:, c, :], start=(c == 0), stop=(c == C - 1))
                m.then_inc(z["v_ready"], 1)

            def scores(b, g):
                wait(pe, z["sub_done"], (b - 1) * G + (g + 1))
                wait(pe, z["q_done"], b + 1)
                wait(pe, z["km_done"], b + 1)
                c, r = g // 2, 64 * (g % 2)
                pe.matmul(SC[g][:], identb[:], causal[:], start=True, stop=False)
                pe.matmul(SC[g][:], qT[r:r + 64, c, :], kM[r:r + 64, c, :, :].rearrange("p e t -> p (e t)"),
                          start=False, stop=True).then_inc(z["scores_ready"], 1)

            def transp(b, g):
                wait(pe, z["exp_done"], b * G + (g + 1))
                wait(pe, z["norm_done"], b * G + (g - 1))
                for n in range(GH):
                    m = pe.transpose(PB[g % 2][:, n * S:(n + 1) * S], P[:, g, n, :], ident[:])
                m.then_inc(z["pt_ready"], 1)

            def pv(b, g, par):
                wait(pe, z["pt_done"], b * G + (g + 1))
                wait(pe, z["v_done"], b + 1)
                for n in range(GH):
                    m = pe.matmul(PB[g % 2][:, n * (HD + 1):(n + 1) * (HD + 1)], PT[g % 2][:, n, :],
                                  vaug[par][:, g * GH + n, :], start=True, stop=True)
                m.then_inc(z["pv_ready"], 1)

            def step(i, par, half):
                attn, proj, tail = within(i, 0), within(i, 1), within(i, -1)
                q, qh = 1 - par, (half + 1 if par else half)
                th = half if par else half - 1
                if attn:
                    scores(i, 0)
                    scores(i, 1)
                if within(i, -2):
                    t_rank(i - 2)
                if tail:
                    t_o(i - 1)
                if attn:
                    scores(i, 2)
                    scores(i, 3)
                if tail:
                    t_wo(i - 1)
                if proj:
                    p_xa(i + 1, q, qh)
                if attn:
                    transp(i, 0)
                if proj:
                    p_h(i + 1, q)
                if tail:
                    t_x1T(i - 1, q)
                if attn:
                    pv(i, 0, par)
                if proj:
                    wait(pe, z["h_done"], i + 2)
                    p_qk(i + 1, WqT, "q_ready")
                if attn:
                    transp(i, 1)
                if tail:
                    t_w2(i - 1, q, th)
                if attn:
                    pv(i, 1, par)
                if proj:
                    wait(pe, z["q_done"], i + 2)
                    p_qk(i + 1, WkT, "k_ready")
                if attn:
                    transp(i, 2)
                if tail:
                    t_x2T(i - 1, q)
                if attn:
                    pv(i, 2, par)
                if proj:
                    p_v(i + 1)
                if attn:
                    transp(i, 3)
                if tail:
                    t_lg(i - 1)
                if attn:
                    pv(i, 3, par)

            steps(pe, -1, B + 2, 3, B - 1, step)

            pe.wait_ge(z["selsum_done"], B + 1)
            pe.wait_ge(z["rank_done"], B)
            pe.matmul(M[1][:, 0:E], onesb[:], selsum[:], start=True, stop=True).then_inc(s_cnt, 1)

            pe.wait_ge(s_experts, 16 * 10)
            pe.wait_ge(s_plan, PLAN)

            def xt(t, par, half):
                wait(pe, s_gathered[par], (half + 1) * 16)
                wait(pe, f["xgT_done"], t - 1)
                for c in range(C):
                    m = pe.transpose(XTB[par][:, c * 128:(c + 1) * 128], xg[par][:, c * 128:(c + 1) * 128], ident[:])
                m.then_inc(f["xgT_ready"], 1)

            def gate_up(t, par, e):
                wait(pe, f["xgT_done"], t + 1)
                wait(pe, f["gub_done"], t - 1)
                for c in range(C):
                    m = pe.matmul(GU[par][:], xgT[par][:, c * 128:(c + 1) * 128], Wgu[:, bass.ds(e * (C * 2 * D) + c * 2 * D, 2 * D)],
                                  start=(c == 0), stop=(c == C - 1))
                m.then_inc(f["gu_ready"], 1)

            def ht(t, par):
                wait(pe, f["hh_done"], t + 1)
                wait(pe, f["hhT_done"], t - 1)
                for c in range(C):
                    m = pe.transpose(HTB[par][:, c * 128:(c + 1) * 128], hh[par][:, c * 128:(c + 1) * 128], ident[:])
                m.then_inc(f["hhT_ready"], 1)

            def down(t, par, e):
                wait(pe, f["hhT_done"], t + 1)
                wait(pe, f["yb_done"], t - 1)
                for c in range(C):
                    m = pe.matmul(YB[par][:, 0:H], hhT[par][:, c * 128:(c + 1) * 128], Wd[:, bass.ds(e * (C * H) + c * H, H)],
                                  start=(c == 0), stop=(c == C - 1))
                m.then_inc(f["y_ready"], 1)

            def tstep(t, par, half):
                if within(t, 0, NT):
                    e_up = pe.value_load(tile_e[0:1, bass.ds(t, 1)], min_val=0, max_val=E - 1)
                if within(t, -3, NT):
                    e_down = pe.value_load(tile_e[0:1, bass.ds(t - 3, 1)], min_val=0, max_val=E - 1)
                if within(t, 0, NT):
                    xt(t, par, half)
                if within(t, -3, NT):
                    down(t - 3, 1 - par, e_down)
                if within(t, -2, NT):
                    ht(t - 2, par)
                if within(t, 0, NT):
                    gate_up(t, par, e_up)

            steps(pe, 0, NT + 3, 5, NT, tstep)

        @block.scalar
        def _(act):
            act.wait_ge(s_const, 16 * len(CONSTS))

            def evac(dst, src, ready, done, b, free, free_count):
                wait(act, z[ready], b + 1)
                wait(act, z[free], free_count)
                act.activation(dst, src, ACT.Copy).then_inc(z[done], 1)

            def exps(b, g):
                wait(act, z["sub_done"], b * G + (g + 1))
                p = P[:, g].rearrange("q h t -> q (h t)")
                act.activation(p, p, ACT.Exp).then_inc(z["exp_done"], 1)

            def pt(b, g):
                wait(act, z["pt_ready"], b * G + (g + 1))
                wait(act, z["pv_ready"], b * G + (g - 1))
                act.activation(PT[g % 2][:].rearrange("q h t -> q (h t)"), PB[g % 2][:], ACT.Copy)\
                    .then_inc(z["pt_done"], 1)

            def biased(dst, bias, ready, done, b):
                wait(act, z[ready], b + 1)
                for c in range(C):
                    m = act.activation(dst[:, c, :], M[1][:, c * S:(c + 1) * S], ACT.Identity, bias=bias[:, c:c + 1])
                m.then_inc(z[done], 1)

            def two(t):
                return t[:].rearrange("p c t -> p (c t)")

            def step(i, par, half):
                attn, proj, tail = within(i, 0), within(i, 1), within(i, -1)
                if attn:
                    exps(i, 0)
                if tail:
                    evac(two(oT), M[0][:, 0:C * S], "oT_ready", "oT_done", i - 1, "x1_ready", i - 1)
                if attn:
                    exps(i, 1)
                    exps(i, 2)
                    pt(i, 0)
                if proj:
                    evac(two(hT), M[1][:, 0:C * S], "h_ready", "h_done", i + 1, "v_ready", i + 1)
                if tail:
                    evac(two(x1T), M[0][:, 0:C * S], "x1T_ready", "x1T_done", i - 1, "x2_ready", i - 1)
                if attn:
                    exps(i, 3)
                if proj:
                    wait(act, z["scores_ready"], (i + 1) * G)
                    biased(qT, bq, "q_ready", "q_done", i + 1)
                if attn:
                    pt(i, 1)
                if proj:
                    wait(act, z["km_done"], i + 1)
                    biased(kT, bk, "k_ready", "k_done", i + 1)
                if attn:
                    pt(i, 2)
                if tail:
                    evac(two(x2T), M[0][:, 0:C * S], "x2T_ready", "x2T_done", i - 1, "lg_ready", i - 1)
                if attn:
                    pt(i, 3)
                if tail:
                    wait(act, z["dtop_done"], i)
                    wait(act, z["pair_done"], i - 1)
                    act.activation(etop[:], dtop[:], ACT.Exp).then_inc(z["etop_done"], 1)

            steps(act, -1, B + 1, 3, B - 1, step)

            def xt_out(t, par):
                wait(act, f["xgT_ready"], t + 1)
                wait(act, f["gu_ready"], t - 1)
                act.activation(xgT[par], XTB[par][:, 0:C * 128], ACT.Copy).then_inc(f["xgT_done"], 1)

            def tstep(t, par, half):
                if within(t, -2, NT):
                    wait(act, f["hhT_ready"], t - 1)
                    wait(act, f["y_ready"], t - 3)
                    act.activation(hhT[par], HTB[par][:, 0:C * 128], ACT.Copy).then_inc(f["hhT_done"], 1)
                if within(t, 1, NT):
                    xt_out(t + 1, 1 - par)
                if within(t, 0, NT):
                    wait(act, f["gclip_done"], t + 1)
                    wait(act, f["hh_done"], t - 1)
                    act.activation(sg[par][:], gu[par][:, 0, :], ACT.Sigmoid, scale=ALPHA).then_inc(f["sig_done"], 1)
                if within(t, -2, NT):
                    wait(act, f["yb_done"], t - 1)
                    wait(act, f["ids_done"], t - 1)
                    wait(act, s_added, (t - 3) * 16)
                    act.activation(yw[par][:], yb[par][:], ACT.Copy, scale=ids[par][:, 1:2].bitcast(F32))\
                        .then_inc(f["yw_done"], 1)

            xt_out(0, 0)
            steps(act, 0, NT + 2, 6, NT - 1, tstep)

        @block.vector
        def _(dve):
            dve.memset(selsum[:], 0.0).then_inc(z["selsum_done"], 1)
            for i in range(2):
                last = dve.memset(vaug[i][:, :, HD:HD + 1], 1.0)
            dve.wait_ge(s_const, 16 * len(CONSTS))

            def heads(ap):
                return ap.rearrange("q (h d) -> q h d", h=NH)

            def softmax(b, g):
                wait(dve, z["scores_ready"], b * G + (g + 1))
                sc = SC[g][:].rearrange("q (h t) -> q h t", h=GH)
                dve.tensor_reduce(out=nmax[:, g], in_=sc, axis=AX.X, op=ALU.max, negate=True).then_inc(z["max_done"], 1)
                wait(dve, z["max_done"], b * G + (g + 1))
                wait(dve, z["pt_ready"], (b - 1) * G + (g + 1))
                dve.tensor_tensor(out=P[:, g], in0=sc, in1=nmax[:, g].unsqueeze(2).broadcast_to([S, GH, S]), op=ALU.add)\
                    .then_inc(z["sub_done"], 1)

            def norm(b, g):
                wait(dve, z["pv_ready"], b * G + (g + 1))
                pvo = PB[g % 2][:, 0:GH * (HD + 1)].rearrange("q (n d) -> q n d", d=HD + 1)
                dve.reciprocal(rsum[:, g % 2, :], pvo[:, :, HD]).then_inc(z["rsum_done"], 1)
                wait(dve, z["rsum_done"], b * G + (g + 1))
                wait(dve, z["oT_ready"], b)
                dve.tensor_tensor(out=o[:, g * GH:(g + 1) * GH, :], in0=pvo[:, :, 0:HD],
                                  in1=rsum[:, g % 2, :].unsqueeze(2).broadcast_to([S, GH, HD]), op=ALU.mult)\
                    .then_inc(z["norm_done"], 1)

            def x1_out(b, par, half):
                wait(dve, z["x1_ready"], b + 1)
                wait(dve, z["xb_done"], b + 1)
                wait(dve, s_x1_stored[par], half * 16)
                wait(dve, z["x1T_ready"], b - 1)
                dve.tensor_tensor(out=x1[par][:], in0=M[1][:, 0:H], in1=xb[:], op=ALU.add).then_inc(z["x1_done"], 1)

            def x2_out(b, par, half):
                wait(dve, z["x2_ready"], b + 1)
                wait(dve, s_x2_stored[par], half * 16)
                wait(dve, s_late[par], (half + 1) * 48)
                wait(dve, z["x2T_ready"], b - 1)
                dve.tensor_tensor(out=x2[par][:], in0=M[0][:, 0:H], in1=b2[par][:], op=ALU.add).then_inc(z["x2_done"], 1)

            def xa_out(b, par, half):
                wait(dve, z["xa_ready"], b + 1)
                wait(dve, s_early[par], (half + 1) * 64)
                wait(dve, z["h_ready"], b)
                dve.tensor_scalar(out=xa[:], in0=M[0][0:RANK, 0:S], scalar1=scal[par][:, 0:1], scalar2=None, op0=ALU.mult)\
                    .then_inc(z["xa_done"], 1)

            def v_out(b, par):
                wait(dve, z["v_ready"], b + 1)
                wait(dve, z["pv_ready"], (b - 1) * G)
                dve.tensor_tensor(out=vaug[par][:, :, 0:HD], in0=heads(M[1][:, 0:H]), in1=heads(bv[:]), op=ALU.add)\
                    .then_inc(z["v_done"], 1)

            def choose(b):
                wait(dve, z["lg_ready"], b + 1)
                dve.tensor_tensor(out=lg[:], in0=M[0][:, 0:E], in1=rbias[:], op=ALU.add).then_inc(z["lg_done"], 1)
                stand_alone(dve, (z["lg_done"], b + 1), (z["etop_done"], b))
                dve.max(out=top8[:], in_=lg[:]).then_inc(z["top_done"], 1)
                stand_alone(dve, (z["top_done"], b + 1))
                dve.max_index(out=topi[:], in_max=top8[:], in_values=lg[:]).then_inc(z["topi_done"], 1)
                dve.tensor_scalar(out=dtop[:], in0=top8[:, 0:TOPK], scalar1=top8[:, 0:1], scalar2=None, op0=ALU.subtract)\
                    .then_inc(z["dtop_done"], 1)
                wait(dve, z["topi_done"], b + 1)
                dve.tensor_copy(topf[:], topi[:, 0:TOPK]).then_inc(z["topf_done"], 1)
                wait(dve, z["topf_done"], b + 1)
                dve.tensor_tensor(out=onehot[:], in0=topf[:].unsqueeze(2).broadcast_to([S, TOPK, E]),
                                  in1=iota_e[:].unsqueeze(1).broadcast_to([S, TOPK, E]), op=ALU.is_equal)\
                    .then_inc(z["onehot_done"], 1)
                wait(dve, z["onehot_done"], b + 1)
                wait(dve, z["rank_ready"], b)
                with nc.allow_low_precision(reason="ones and zeros"):
                    dve.tensor_reduce(out=sel[:], in_=onehot[:].rearrange("p j e -> p e j"), axis=AX.X, op=ALU.add)\
                        .then_inc(z["sel_done"], 1)

            def ranked(b):
                wait(dve, z["rank_ready"], b + 1)
                dve.tensor_tensor(out=rank[:], in0=M[1][:, 0:E], in1=ebase[:], op=ALU.add).then_inc(z["rank_done"], 1)
                dve.tensor_tensor(out=selsum[:], in0=selsum[:], in1=sel[:], op=ALU.add).then_inc(z["selsum_done"], 1)

            def place(b, par, half):
                wait(dve, z["rank_done"], b + 1)
                dve.tensor_tensor(out=prod[:], in0=onehot[:], in1=rank[:].unsqueeze(1).broadcast_to([S, TOPK, E]),
                                  op=ALU.mult).then_inc(z["prod_done"], 1)
                wait(dve, z["etop_done"], b + 1)
                dve.tensor_reduce(out=esum[:], in_=etop[:], axis=AX.X, op=ALU.add).then_inc(z["esum_done"], 1)
                wait(dve, z["prod_done"], b + 1)
                with nc.allow_low_precision(reason="whole numbers below 2^24"):
                    dve.tensor_reduce(out=slot[:], in_=prod[:], axis=AX.X, op=ALU.add).then_inc(z["slot_done"], 1)
                wait(dve, z["esum_done"], b + 1)
                dve.reciprocal(einv[:], esum[:]).then_inc(z["einv_done"], 1)
                wait(dve, z["slot_done"], b + 1)
                dve.tensor_scalar(out=slot_p[:], in0=slot[:], scalar1=127, scalar2=None, op0=ALU.bitwise_and)\
                    .then_inc(z["slotp_done"], 1)
                dve.tensor_scalar(out=slot_c[:], in0=slot[:], scalar1=7, scalar2=None, op0=ALU.arith_shift_right)\
                    .then_inc(z["slotc_done"], 1)
                wait(dve, s_scattered[par], half * (16 * TOPK))
                wait(dve, z["einv_done"], b + 1)
                dve.tensor_scalar(out=pair[par][:, :, 1].bitcast(F32), in0=etop[:], scalar1=einv[:, 0:1], scalar2=None,
                                  op0=ALU.mult)
                dve.tensor_scalar(out=pair[par][:, :, 0], in0=pair[par][:, :, 0], scalar1=float(2 * S), scalar2=None,
                                  op0=ALU.add).then_inc(z["pair_done"], 1)
                wait(dve, z["slotp_done"], b + 1)
                wait(dve, z["slotc_done"], b + 1)
                dve.scalar_tensor_tensor(out=slot_row[par][:], in0=slot_p[:], scalar=float(TCOLS), in1=slot_c[:],
                                         op0=ALU.mult, op1=ALU.add).then_inc(z["slotrow_done"], 1)

            def step(i, par, half):
                attn, proj, tail = within(i, 0), within(i, 1), within(i, -1)
                q, qh = 1 - par, (half + 1 if par else half)
                th = half if par else half - 1
                if attn:
                    softmax(i, 0)
                if within(i, -2):
                    ranked(i - 2)
                if attn:
                    softmax(i, 1)
                    softmax(i, 2)
                if tail:
                    x1_out(i - 1, q, th)
                if proj:
                    xa_out(i + 1, q, qh)
                if attn:
                    softmax(i, 3)
                if within(i, -2):
                    place(i - 2, par, half - 1)
                if attn:
                    norm(i, 0)
                if tail:
                    x2_out(i - 1, q, th)
                if attn:
                    norm(i, 1)
                    norm(i, 2)
                if proj:
                    v_out(i + 1, q)
                if tail:
                    choose(i - 1)
                if attn:
                    norm(i, 3)

            steps(dve, -1, B + 2, 5, B - 1, step)

            dve.wait_ge(s_cnt, 1)
            n = [0]

            def then(m):
                m.then_inc(s_plan, 1)
                n[0] += 1
                dve.wait_ge(s_plan, n[0])

            def tiles_of(ap):
                return ap.unsqueeze(1).broadcast_to([1, NT, E])

            then(dve.memset(one_e[:], 1.0))
            then(dve.tensor_scalar(out=cnt[:], in0=M[1][0:1, 0:E], scalar1=127.0, scalar2=None, op0=ALU.add))
            then(dve.tensor_scalar(out=ntile[:], in0=cnt[:], scalar1=7, scalar2=None, op0=ALU.arith_shift_right))
            then(dve.tensor_copy(ntilef[:], ntile[:]))
            then(dve.tensor_tensor_scan(out=cum[:], data0=one_e[:], data1=ntilef[:], initial=0.0, op0=ALU.mult, op1=ALU.add))
            then(dve.tensor_tensor(out=past, in0=iota_t[:].unsqueeze(2).broadcast_to([1, NT, E]), in1=tiles_of(cum[:]),
                                   op=ALU.is_ge))
            then(dve.tensor_reduce(out=t_e[:], in_=past, axis=AX.X, op=ALU.add))
            then(dve.tensor_tensor(out=past, in0=past, in1=tiles_of(ntilef[:]), op=ALU.mult))
            then(dve.tensor_reduce(out=t_s[:], in_=past, axis=AX.X, op=ALU.add))
            then(dve.scalar_tensor_tensor(out=t_r[:], in0=t_e[:], scalar=float(RT), in1=iota_t[:], op0=ALU.mult, op1=ALU.add))
            then(dve.tensor_tensor(out=t_r[:], in0=t_r[:], in1=t_s[:], op=ALU.subtract))
            then(dve.tensor_scalar(out=tile_c[:], in0=t_r[:], scalar1=float(TCOLS - 1), scalar2=None, op0=ALU.min))
            then(dve.tensor_scalar(out=tile_e[:], in0=t_e[:], scalar1=float(E - 1), scalar2=None, op0=ALU.min))
            assert n[0] == PLAN

            dve.wait_ge(s_experts, 16 * 10)

            def tstep(t, par, half):
                if within(t, 0, NT):
                    e_up = dve.value_load(tile_e[0:1, bass.ds(t, 1)], min_val=0, max_val=E - 1)
                if within(t, -2, NT):
                    e_down = dve.value_load(tile_e[0:1, bass.ds(t - 2, 1)], min_val=0, max_val=E - 1)
                if within(t, 0, NT):
                    wait(dve, f["gu_ready"], t + 1)
                    g2 = gu[par][:].rearrange("p k d -> p (k d)")
                    dve.tensor_tensor(out=g2, in0=GU[par][:], in1=bgu[:, bass.ds(e_up * (2 * D), 2 * D)], op=ALU.add)\
                        .then_inc(f["gub_done"], 1)
                    wait(dve, f["gub_done"], t + 1)
                    dve.tensor_scalar(out=gu[par][:, 0, :], in0=gu[par][:, 0, :], scalar1=LIMIT, scalar2=None, op0=ALU.min)\
                        .then_inc(f["gclip_done"], 1)
                    dve.tensor_scalar(out=gu[par][:, 1, :], in0=gu[par][:, 1, :], scalar1=LIMIT, scalar2=-LIMIT,
                                      op0=ALU.min, op1=ALU.max).then_inc(f["uclip_done"], 1)
                if within(t, -2, NT):
                    wait(dve, f["y_ready"], t - 1)
                    wait(dve, f["yw_done"], t - 3)
                    dve.tensor_tensor(out=yb[par][:], in0=YB[par][:, 0:H], in1=bd[:, bass.ds(e_down * H, H)], op=ALU.add)\
                        .then_inc(f["yb_done"], 1)
                if within(t, 0, NT):
                    wait(dve, f["sig_done"], t + 1)
                    dve.tensor_tensor(out=sg[par][:], in0=sg[par][:], in1=gu[par][:, 0, :], op=ALU.mult)\
                        .then_inc(f["glu_done"], 1)
                    wait(dve, f["glu_done"], t + 1)
                    wait(dve, f["uclip_done"], t + 1)
                    wait(dve, f["hhT_ready"], t - 1)
                    dve.scalar_tensor_tensor(out=hh[par][:], in0=gu[par][:, 1, :], scalar=1.0, in1=sg[par][:],
                                             op0=ALU.add, op1=ALU.mult).then_inc(f["hh_done"], 1)

            steps(dve, 0, NT + 2, 6, NT - 1, tstep)


PLAN = 13


def kernel(**inputs):
    import numpy as np
    import ml_dtypes
    import concourse.bacc as bacc
    from concourse.bass_utils import run_bass_kernel_spmd

    v = {k: np.asarray(x) for k, x in inputs.items()}
    bf = ml_dtypes.bfloat16

    def chunked(w):
        return w.reshape(-1, 128, w.shape[-1]).transpose(1, 0, 2)

    def apart(w):
        return np.concatenate([w[..., ::2], w[..., 1::2]], -1)

    p = np.arange(128)
    q, k = p[:, None], p[None, :]
    mask = np.where(k <= q, 0.0, -2.0 ** 100)
    table = np.zeros((128, TCOLS, 2), np.int32)
    table[:, :, 0] = ROWS + q
    pair = np.zeros((2, 128, TOPK, 2), np.int32)
    pair[:, :, :, 0] = (p[:, None] + 128 * np.arange(2)[:, None, None] - 2 * S)
    arrays = {
        "idx": np.concatenate([v["itok_B_0_6"], v["itok_B_0_15"]]).reshape(1, 2 * B),
        "xT": v["x"].reshape(B, S, C, 128).transpose(0, 3, 2, 1),
        "x": v["x"],
        "AT": v["L0_cond_A"].reshape(8, RANK, C, 128).transpose(0, 3, 2, 1),
        "BT": v["L0_cond_Bm"].transpose(0, 2, 1),
        "scal": v["L0_cond_scalings"],
        "W2": v["L0_cond2_W"].reshape(E, C, 128, H).transpose(0, 2, 1, 3),
        "b2": v["L0_cond2_b"],
        "WT": chunked(v["L0_cond_W"].T),
        "WqT": chunked(v["L0_attn_Wq"].T),
        "WkT": chunked(v["L0_attn_Wk"].T),
        "WvT": chunked(v["L0_attn_Wv"].T),
        "WoT": chunked(v["L0_attn_Wo"].T),
        "RWT": chunked(v["L0_ffn_router_weight"].T),
        "bq": v["L0_attn_bq"].reshape(C, 128).T,
        "bk": v["L0_attn_bk"].reshape(C, 128).T,
        "bv": v["L0_attn_bv"],
        "bo": v["L0_attn_bo"],
        "rbias": v["L0_ffn_router_bias"],
        "Wgu": apart(v["L0_ffn_gate_up_proj"]).reshape(E, C, 128, 2 * D).transpose(2, 0, 1, 3).reshape(128, -1),
        "Wd": v["L0_ffn_down_proj"].reshape(E, C, 128, H).transpose(2, 0, 1, 3).reshape(128, -1),
        "bgu": apart(v["L0_ffn_gate_up_proj_bias"]).reshape(-1),
        "bd": v["L0_ffn_down_proj_bias"].reshape(-1),
        "ident": np.eye(128, dtype=np.float32),
        "identb": np.eye(128).astype(bf),
        "causal": np.tile(mask, (1, GH)).astype(bf),
        "tri": (q < k).astype(bf),
        "onesb": np.ones((128, 128), bf),
        "iota_e": np.tile(np.arange(E, dtype=np.float32), (128, 1)),
        "ebase": np.tile(np.arange(E, dtype=np.float32) * ROWS, (128, 1)),
        "iota_t": np.arange(NT, dtype=np.float32).reshape(1, NT),
        "kmask": ((p[:, None] % 64) // HD == np.arange(GH)).astype(np.float32) / np.float32(HD ** 0.5),
        "table": table.reshape(128, -1),
        "pair0": pair[0],
        "pair1": pair[1],
    }
    nc = bacc.Bacc("TRN2", target_bir_lowering=False, num_devices=1)
    feeds, aps = {}, {}
    for name, arr in arrays.items():
        arr = np.ascontiguousarray(arr)
        feeds[f"in_{name}"] = arr
        aps[name] = nc.dram_tensor(f"in_{name}", arr.shape, mybir.dt.from_np(arr.dtype), kind="ExternalInput").ap()
    out = nc.dram_tensor("out_rows", (ROWS + PADROWS, H), F32, kind="ExternalOutput").ap()
    adaln_attn_moe(nc, aps, out)
    r = run_bass_kernel_spmd(nc, [feeds], core_ids=[0])
    return r.results[0]["out_rows"][:ROWS].reshape(B, S, H)
```

```python
import concourse.bass as bass
from concourse import mybir
from contextlib import ExitStack

F32 = mybir.dt.float32
BF16 = mybir.dt.bfloat16
I32 = mybir.dt.int32
U32 = mybir.dt.uint32
ALU = mybir.AluOpType
ACT = mybir.ActivationFunctionType
AX = mybir.AxisListType

B = 16
S = 128
H = 256
C = H // 128
NH = 16
HD = H // NH
G = 4
GH = NH // G
CH = NH // C
RANK = 16
E = 16
D = 256
TOPK = 4
ALPHA = 1.702
LIMIT = 7.0
ROWS = B * S
NT = ROWS * TOPK // 128 + E - 1
RT = ROWS // 128
WE = C * 2 * D + C * H
BE = 2 * D + H
PAIRS = (NT + 3) // 2
TCOLS = E * RT + 1
PADROWS = 128


def adaln_attn_moe(nc: bass.Bass, a, out):
    ctx = ExitStack()
    with ctx:
        def sb(name, shape, dt=F32):
            return ctx.enter_context(nc.sbuf_tensor(name, shape, dt))

        def ps(name, dt=F32):
            return ctx.enter_context(nc.psum_tensor(name, [128, 512], dt))

        def sem(name):
            return ctx.enter_context(nc.semaphore(name))

        x2_rows = nc.dram_tensor("x2_rows", [ROWS + PADROWS, H], F32, kind="Internal").ap()
        slot_table = nc.dram_tensor("slot_table", [128 * TCOLS, 2], I32, kind="Internal").ap()
        table_by_row = slot_table.rearrange("(p c) two -> p (c two)", c=TCOLS)

        small = sb("small", [128, 128 + 2 * E + CH + 2 * C + C * E + 1])
        at = [0]

        def part(width):
            at[0] += width
            return small[:, at[0] - width:at[0]]

        ident = part(128)
        iota_e = part(E)
        ebase = part(E)
        kmask = part(CH)
        bq = part(C)
        bk = part(C)
        RWT = part(C * E).rearrange("p (c e) -> p c e", e=E)
        tile_id = part(1)
        patterns = sb("patterns", [128, (GH + 2) * 128], BF16)
        causal = patterns[:, 0:GH * 128]
        tri = patterns[:, GH * 128:(GH + 1) * 128]
        onesb = patterns[:, (GH + 1) * 128:(GH + 2) * 128]
        biases = sb("biases", [128, 2 * H + E])
        bv = biases[:, 0:H]
        bo = biases[:, H:2 * H]
        rbias = biases[:, 2 * H:2 * H + E]
        idx = sb("idx", [1, 2 * B], I32)
        WT = sb("WT", [128, C, H])
        WqT = sb("WqT", [128, C, H])
        WkT = sb("WkT", [128, C, H])
        WvT = sb("WvT", [128, C, H])
        WoT = sb("WoT", [128, C, H])

        xT = [sb(f"xT{i}", [128, C, S]) for i in range(2)]
        AT = [sb(f"AT{i}", [128, C, RANK]) for i in range(2)]
        BT = [sb(f"BT{i}", [RANK, H + 1]) for i in range(2)]
        xrow = [sb(f"xrow{i}", [S, H]) for i in range(2)]
        W2 = [sb(f"W2_{i}", [128, C, H]) for i in range(2)]
        b2 = [sb(f"b2_{i}", [S, H]) for i in range(2)]
        xa = sb("xa", [RANK, S])
        hT = sb("hT", [128, C, S])
        qT = sb("qT", [128, C, S])
        kT = sb("kT", [128, C, S])
        kM = sb("kM", [128, C, CH, S])
        vaug = [sb(f"vaug{i}", [S, NH, HD + 1]) for i in range(2)]
        P = sb("P", [S, G, GH, S])
        nmax = sb("nmax", [S, G, GH])
        PT = [sb(f"PT{i}", [S, GH, S]) for i in range(2)]
        rsum = sb("rsum", [S, 2, GH])
        o = sb("o", [S, NH, HD])
        oT = sb("oT", [128, C, S])
        xb = sb("xb", [S, H])
        x1 = [sb(f"x1_{i}", [S, H]) for i in range(2)]
        x1T = sb("x1T", [128, C, S])
        x2 = [sb(f"x2_{i}", [S, H]) for i in range(2)]
        x2T = sb("x2T", [128, C, S])
        lg = sb("lg", [S, E])
        top8 = sb("top8", [S, 8])
        topi = sb("topi", [S, 8], U32)
        topf = sb("topf", [S, TOPK])
        onehot = sb("onehot", [S, TOPK, E])
        sel = sb("sel", [S, E], BF16)
        selsum = sb("selsum", [S, E], BF16)
        rank = sb("rank", [S, E])
        prod = sb("prod", [S, TOPK, E])
        slot = sb("slot", [S, TOPK], I32)
        slot_p = sb("slot_p", [S, TOPK], I32)
        slot_c = sb("slot_c", [S, TOPK], I32)
        slot_row = [sb(f"slot_row{i}", [S, TOPK], I32) for i in range(2)]
        pairs = sb("pairs", [S, 2 * TOPK * 2], I32)
        pair = [pairs[:, i * 2 * TOPK:(i + 1) * 2 * TOPK].rearrange("p (j two) -> p j two", two=2) for i in range(2)]
        dtop = sb("dtop", [S, TOPK])
        etop = sb("etop", [S, TOPK])
        esum = sb("esum", [S, 1])
        einv = sb("einv", [S, 1])

        We = sb("We", [128, E * WE])
        be = sb("be", [128, E * BE])
        table = kM[:].rearrange("p c h t -> p (c h t)")[:, 0:TCOLS * 2].bitcast(I32)
        zrow = xb
        scratch = sb("scratch", [128, 1])

        cnt = sb("cnt", [128, E], I32)
        ntile = sb("ntile", [128, E], I32)
        ntilef, cum = prod[:, 0], prod[:, 1]
        one_e = sb("one_e", [128, E])
        past = prod[:, 2]
        t_e = sb("t_e", [128, 1])
        t_s = sb("t_s", [128, 1])
        t_r = sb("t_r", [128, 1])
        tile_of = sb("tile_of", [128, 2])
        old_scores = P[0:1].rearrange("p g h s -> p (g h s)").bitcast(I32)
        plan_e = old_scores[:, 0:PAIRS * 4]
        plan_c = old_scores[:, 256:256 + PAIRS * 4]
        plan_p = old_scores[:, 512:512 + (PAIRS + 1) * 4]

        idg = [sb(f"idg{i}", [128, 2], I32) for i in range(2)]
        ids = [sb(f"ids{i}", [128, 2], I32) for i in range(2)]
        zeros = hT[:].rearrange("p c t -> p (c t)").bitcast(BF16)
        def halves(t):
            w = t[:].rearrange("p c n -> p (c n)")
            return [w[:, 0:H], w[:, H:2 * H]]

        xg = halves(WvT)
        xgT = halves(PT[0])
        gu = [P[:, 2 + i].rearrange("p h s -> p (h s)").rearrange("p (k d) -> p k d", k=2) for i in range(2)]
        hhT = halves(PT[1])
        hh = halves(W2[0])
        sg = halves(W2[1])
        yb = halves(WqT)
        yw = halves(WkT)

        bank = [ps(f"bank{i}") for i in range(8)]
        SC = bank[0:4]
        PB = bank[4:6]
        M = bank[6:8]
        GU = bank[0:2]
        XTB = bank[2:4]
        HTB = bank[4:6]
        YB = bank[6:8]

        s_first = sem("first_constants_loaded")
        s_wk = sem("key_weights_loaded")
        s_qv = sem("other_projection_constants_loaded")
        s_rest = sem("other_constants_loaded")
        s_idx = sem("idx_loaded")
        s_early = [sem(f"early_loaded{i}") for i in range(2)]
        s_late = [sem(f"late_loaded{i}") for i in range(2)]
        s_experts = sem("experts_loaded")
        s_init = sem("init_done")
        s_zeros = sem("zeros_written")
        s_tinit = sem("table_init_stored")
        names = ("xa_ready xa_done h_ready h_done q_ready q_done k_ready k_done v_ready v_done scores_ready "
                 "km_done mask_done max_done exp_done pt_ready pt_done pv_ready rsum_done norm_done oT_ready oT_done "
                 "x1_ready x1_done x1T_ready x1T_done x2_ready x2_done x2T_ready x2T_done lg_ready lg_done "
                 "xb_done top_done topi_done topf_done onehot_done sel_done rank_ready rank_done prod_done "
                 "slot_done slotp_done slotc_done slotrow_done dtop_done etop_done esum_done einv_done "
                 "pair_done selsum_done").split()
        z = {n: sem(n) for n in names}
        s_x1_stored = [sem(f"x1_stored{i}") for i in range(2)]
        s_x2_stored = [sem(f"x2_stored{i}") for i in range(2)]
        s_scattered = [sem(f"pairs_scattered{i}") for i in range(2)]
        s_pad = sem("pad_rows_stored")
        s_passed = sem("waits_passed")
        s_cnt = sem("counts_ready")
        s_plan = sem("plan_steps")
        s_planrow = sem("plan_on_one_row")
        s_table = sem("table_loaded")
        s_gathered = [sem(f"rows_gathered{i}") for i in range(2)]
        s_added = sem("rows_added")
        names = ("idg_done ids_done xgT_ready xgT_done gu_ready gub_done gclip_done uclip_done sig_done glu_done "
                 "hh_done hhT_ready hhT_done y_ready yb_done yw_done").split()
        f = {n: sem(n) for n in names}

        def wait(eng, s, value):
            if not isinstance(value, int) or value > 0:
                eng.wait_ge(s, value)

        def stand_alone(eng, *waits):
            for s, v in waits:
                wait(eng, s, v)
            eng.sem_inc(s_passed, 1)

        def steps(eng, lo, hi, full_lo, full_hi, body):
            for t in range(lo, full_lo):
                body(t, t % 2, t // 2)
            with eng.Fori(0, (full_hi - full_lo) // 2) as j:
                for u in range(2):
                    body(j * 2 + (full_lo + u), (full_lo + u) % 2, j + (full_lo + u) // 2)
            for t in range(full_hi, hi):
                body(t, t % 2, t // 2)

        def numbers(eng, engine, plan, top, row):
            _, v = nc.values_load_multi_w_load_instructions(
                plan[0:1, bass.ds(row * 4, 4)], engines=(engine,), min_val=0, max_val=top,
                skip_runtime_bounds_check_because="the plan keeps its numbers in this range")
            return v

        def tile_steps(eng, engine, plan, top, ahead, full, hi, body):
            def pair_of(first, k, ts):
                v = numbers(eng, engine, plan, top, k)
                for u in ts:
                    body(first + u, (u + ahead) % 2, k + (u - ahead) // 2, v[u], v[2 + u])
            for k in range(3):
                pair_of(2 * k - ahead, k, [u for u in (0, 1) if 2 * k - ahead + u >= 0])
            with eng.Fori(0, full - 3) as j:
                pair_of(j * 2 + (6 - ahead), j + 3, (0, 1))
            for k in range(full, (hi + ahead + 1) // 2):
                pair_of(2 * k - ahead, k, [u for u in (0, 1) if 2 * k - ahead + u < hi])

        def within(t, off, n=B):
            return not isinstance(t, int) or 0 <= t + off < n

        block = ctx.enter_context(nc.Block())

        @block.sync
        def _(sp):
            sp.dma_start(idx[:, :], a["idx"]).then_inc(s_idx, 16)

            def early(b, par, half):
                wait(sp, z["h_ready"], b - 1)
                sp.dma_start(xT[par][:], a["xT"][bass.ds(b, 1)].rearrange("o p c t -> (o p) c t")).then_inc(s_early[par], 16)
                if isinstance(b, int) and b == 0:
                    sp.dma_start(WT[:], a["WT"]).then_inc(s_first, 16)
                    sp.dma_start(small[:], a["small"]).then_inc(s_first, 16)
                    sp.wait_ge(s_idx, 16)
                ad = sp.value_load(idx[0:1, bass.ds(b, 1)], min_val=0, max_val=7)
                sp.dma_start(AT[par][:], a["AT"][bass.ds(ad, 1)].rearrange("o p c r -> (o p) c r")).then_inc(s_early[par], 16)
                sp.dma_start(BT[par][:], a["BT"][bass.ds(ad, 1)].rearrange("o r h -> (o r) h")).then_inc(s_early[par], 16)

            def late(b, par, half):
                wait(sp, z["x2_done"], b - 1)
                wait(sp, z["xb_done"], b - 1)
                ex = sp.value_load(idx[0:1, bass.ds(b + B, 1)], min_val=0, max_val=E - 1)
                sp.dma_start(xrow[par][:], a["x"][bass.ds(b, 1)].rearrange("o t h -> (o t) h")).then_inc(s_late[par], 16)
                sp.dma_start(W2[par][:], a["W2"][bass.ds(ex, 1)].rearrange("o p c h -> (o p) c h")).then_inc(s_late[par], 16)
                sp.dma_start(b2[par][:], a["b2"][bass.ds(ex, 1)].rearrange("o h -> (o h)").partition_broadcast(S)).then_inc(s_late[par], 16)

            def store(b, par, half):
                wait(sp, z["x1_done"], b + 1)
                sp.dma_start(out[bass.ds(b * S, S)], x1[par][:]).then_inc(s_x1_stored[par], 16)
                wait(sp, z["x2_done"], b + 1)
                sp.dma_start(x2_rows[bass.ds(b * S, S)], x2[par][:]).then_inc(s_x2_stored[par], 16)

            def expert(e):
                sp.dma_start(We[:, bass.ds(e * WE, WE)], a["experts"][bass.ds(e, 1)].rearrange("o p w -> (o p) w"))\
                    .then_inc(s_experts, 16)
                sp.dma_start(be[:, bass.ds(e * BE, BE)],
                             a["expert_biases"][bass.ds(e, 1)].rearrange("o w -> (o w)").partition_broadcast(128))\
                    .then_inc(s_experts, 16)

            early(0, 0, 0)
            for dst, name, loaded in ((WkT, "WkT", s_wk), (patterns, "patterns", s_wk), (WqT, "WqT", s_qv), (WvT, "WvT", s_qv)):
                sp.dma_start(dst[:], a[name]).then_inc(loaded, 16)
            sp.dma_start(biases[:], a["biases"].partition_broadcast(128)).then_inc(s_qv, 16)
            early(1, 1, 0)
            sp.dma_start(WoT[:], a["WoT"]).then_inc(s_rest, 16)
            sp.dma_start(pairs[:], a["pairs"]).then_inc(s_rest, 16)
            late(0, 0, 0)
            sp.dma_start(table_by_row, a["table"]).then_inc(s_tinit, 16)
            sp.wait_ge(s_init, 2)
            sp.dma_start(x2_rows[ROWS:ROWS + PADROWS], zrow[:]).then_inc(s_pad, 16)
            sp.dma_start(out[ROWS:ROWS + PADROWS], zrow[:]).then_inc(s_pad, 16)

            def step(i, par, half):
                if within(i, 2):
                    early(i + 2, par, half + 1)
                if within(i, 0, E):
                    expert(i)
                if within(i, -1):
                    store(i - 1, 1 - par, half if par else half - 1)
                if within(i, 1):
                    late(i + 1, 1 - par, half + 1 if par else half)

            steps(sp, 0, B + 1, 1, 13, step)

            for par in range(2):
                sp.wait_ge(s_scattered[par], 16 * TOPK * (B // 2))
            sp.dma_start(table[:, :], table_by_row).then_inc(s_table, 16)
            sp.wait_ge(s_added, 16 * NT)

        @block.gpsimd
        def _(pool):
            pool.memset(zrow[:], 0.0).then_inc(s_init, 1)
            pool.wait_ge(s_first, 32)
            pool.wait_ge(s_qv, 48)

            def residual(b, par, half):
                wait(pool, s_late[par], (half + 1) * 48)
                if isinstance(b, int) and b == 0:
                    pool.wait_ge(s_pad, 32)
                wait(pool, z["x1_done"], b)
                pool.tensor_tensor(out=xb[:], in0=xrow[par][:], in1=bo[:], op=ALU.add).then_inc(z["xb_done"], 1)

            def mask_k(b):
                wait(pool, z["k_done"], b + 1)
                wait(pool, z["scores_ready"], b * G)
                for c in range(C):
                    pool.tensor_tensor(out=kM[:, c], in0=kT[:, c, :].unsqueeze(1).broadcast_to([128, CH, S]),
                                       in1=kmask[:].unsqueeze(2).broadcast_to([128, CH, S]), op=ALU.mult)\
                        .then_inc(z["km_done"], 1)

            def scatter(b, bp):
                stand_alone(pool, (z["slotrow_done"], b + 1), (z["pair_done"], b + 1))
                if isinstance(b, int) and b == 0:
                    pool.wait_ge(s_tinit, 16)
                for j in range(TOPK):
                    pool.indirect_dma_start(
                        out=slot_table, out_offset=bass.IndirectOffsetOnAxis(ap=slot_row[bp][:, j:j + 1], axis=0),
                        in_=pair[bp][:, j, :], in_offset=None).then_inc(s_scattered[bp], 16)

            def step(i, par, half):
                if within(i, -1):
                    residual(i - 1, 1 - par, half if par else half - 1)
                if within(i, 1):
                    mask_k(i + 1)
                if within(i, -2):
                    scatter(i - 2, par)

            steps(pool, -1, B + 2, 3, B - 1, step)

            pool.wait_ge(s_table, 16)
            pool.wait_ge(s_plan, PLAN)
            for par in range(2):
                pool.wait_ge(s_x2_stored[par], 16 * (B // 2))
                pool.wait_ge(s_x1_stored[par], 16 * (B // 2))
            pool.wait_ge(s_pad, 32)

            def gather(t, par, half, c):
                wait(pool, s_gathered[par], half * 16)
                pool.tensor_copy(idg[par][:], table[:, bass.ds(c * 2, 2)]).then_inc(f["idg_done"], 1)
                stand_alone(pool, (f["idg_done"], t + 1), (f["xgT_ready"], t - 1))
                pool.indirect_dma_start(
                    out=xg[par][:], out_offset=None, in_=x2_rows,
                    in_offset=bass.IndirectOffsetOnAxis(ap=idg[par][:, 0:1], axis=0)).then_inc(s_gathered[par], 16)

            def add(t, par):
                stand_alone(pool, (f["yw_done"], t + 1), (s_added, t * 16))
                pool.indirect_dma_start(
                    out=out, out_offset=bass.IndirectOffsetOnAxis(ap=ids[par][:, 0:1], axis=0),
                    in_=yw[par][:], in_offset=None, compute_op=ALU.add).then_inc(s_added, 16)

            def keep(t, par, c):
                wait(pool, s_added, (t - 1) * 16)
                pool.tensor_copy(ids[par][:], table[:, bass.ds(c * 2, 2)]).then_inc(f["ids_done"], 1)

            for t in range(3):
                first = pool.value_load(plan_c[0:1, FIRST_C[t]:FIRST_C[t] + 1], min_val=0, max_val=TCOLS - 1)
                gather(t, t % 2, t // 2, first)

            def tstep(t, par, half, c_keep, c_gather):
                if within(t, -3, NT):
                    add(t - 3, 1 - par)
                if within(t, -2, NT):
                    keep(t - 2, par, c_keep)
                if within(t, 3, NT):
                    gather(t + 3, 1 - par, half + 2 if par else half + 1, c_gather)

            tile_steps(pool, mybir.EngineType.Pool, plan_c, TCOLS - 1, 0, (NT - 3) // 2, NT + 3, tstep)

        @block.tensor
        def _(pe):
            def keep_busy(n, left, right):
                for _ in range(n):
                    pe.matmul(SC[0][:], left, right, start=True, stop=True)

            def linger(i, first=0, drain=0, last=0):
                if isinstance(i, int):
                    keep_busy({-1: first, B - 1: drain, B: last}.get(i, 0), onesb, causal)

            pe.wait_ge(s_zeros, 1)
            keep_busy(11, zeros[:, 0:128], zeros)
            pe.wait_ge(s_first, 32)

            def t_o(b):
                wait(pe, z["norm_done"], b * G + G)
                wait(pe, z["lg_done"], b)
                of = o[:].rearrange("q h d -> q (h d)")
                for c in range(C):
                    m = pe.transpose(M[0][:, c * S:(c + 1) * S], of[:, c * 128:(c + 1) * 128], ident[:])
                m.then_inc(z["oT_ready"], 1)

            def t_wo(b):
                wait(pe, z["oT_done"], b + 1)
                wait(pe, z["rank_done"], b)
                wait(pe, z["v_done"], b + 2 if within(b, 1) else B)
                for c in range(C):
                    m = pe.matmul(M[1][:, 0:H], oT[:, c, :], WoT[:, c, :], start=(c == 0), stop=(c == C - 1))
                m.then_inc(z["x1_ready"], 1)

            def t_x1T(b, par):
                wait(pe, z["x1_done"], b + 1)
                wait(pe, z["xa_done"], b + 1)
                for c in range(C):
                    m = pe.transpose(M[0][:, c * S:(c + 1) * S], x1[par][:, c * 128:(c + 1) * 128], ident[:])
                m.then_inc(z["x1T_ready"], 1)

            def t_w2(b, par, half):
                wait(pe, s_late[par], (half + 1) * 48)
                wait(pe, z["x1T_done"], b + 1)
                for c in range(C):
                    m = pe.matmul(M[0][:, 0:H], x1T[:, c, :], W2[par][:, c, :], start=(c == 0), stop=(c == C - 1))
                m.then_inc(z["x2_ready"], 1)

            def t_x2T(b, par):
                wait(pe, z["x2_done"], b + 1)
                for c in range(C):
                    m = pe.transpose(M[0][:, c * S:(c + 1) * S], x2[par][:, c * 128:(c + 1) * 128], ident[:])
                m.then_inc(z["x2T_ready"], 1)

            def t_lg(b):
                wait(pe, z["x2T_done"], b + 1)
                for c in range(C):
                    m = pe.matmul(M[0][:, 0:E], x2T[:, c, :], RWT[:, c, :], start=(c == 0), stop=(c == C - 1))
                m.then_inc(z["lg_ready"], 1)

            def t_rank(b):
                wait(pe, z["sel_done"], b + 1)
                wait(pe, z["selsum_done"], b + 1)
                wait(pe, z["v_done"], b + 3 if within(b, 2) else B)
                pe.matmul(M[1][:, 0:E], tri[:], sel[:], start=True, stop=False)
                pe.matmul(M[1][:, 0:E], onesb[:], selsum[:], start=False, stop=True).then_inc(z["rank_ready"], 1)

            def p_xa(b, par, half):
                wait(pe, s_early[par], (half + 1) * 48)
                wait(pe, z["oT_done"], b - 1)
                wait(pe, z["lg_done"], b - 2)
                for c in range(C):
                    m = pe.matmul(M[0][0:RANK, 0:S], AT[par][:, c, :], xT[par][:, c, :], start=(c == 0), stop=(c == C - 1))
                m.then_inc(z["xa_ready"], 1)

            def p_h(b, par):
                wait(pe, z["xa_done"], b + 1)
                wait(pe, z["x1_done"], b - 1)
                wait(pe, z["v_done"], b)
                for k in range(C):
                    dst = M[1][:, k * S:(k + 1) * S]
                    for c in range(C):
                        pe.matmul(dst, WT[:, c, k * 128:(k + 1) * 128], xT[par][:, c, :], start=(c == 0), stop=False)
                    m = pe.matmul(dst, BT[par][:, k * 128:(k + 1) * 128], xa[:], start=False, stop=True)
                m.then_inc(z["h_ready"], 1)

            def p_qk(b, w, ready):
                for k in range(C):
                    for c in range(C):
                        m = pe.matmul(M[1][:, k * S:(k + 1) * S], w[:, c, k * 128:(k + 1) * 128], hT[:, c, :],
                                      start=(c == 0), stop=(c == C - 1))
                m.then_inc(z[ready], 1)

            def p_v(b):
                wait(pe, z["q_done"], b + 1)
                for c in range(C):
                    m = pe.matmul(M[1][:, 0:H], hT[:, c, :], WvT[:, c, :], start=(c == 0), stop=(c == C - 1))
                m.then_inc(z["v_ready"], 1)

            def scores(b, g):
                wait(pe, z["mask_done"], (b - 1) * G + (g + 1))
                wait(pe, z["q_done"], b + 1)
                c, n = g * GH // CH, g * GH % CH
                wait(pe, z["km_done"], b * C + (c + 1))
                pe.matmul(SC[g][:], qT[:, c, :], kM[:, c, n:n + GH, :].rearrange("p e t -> p (e t)"),
                          start=True, stop=True).then_inc(z["scores_ready"], 1)

            def transp(b, g):
                wait(pe, z["exp_done"], b * G + (g + 1))
                wait(pe, z["norm_done"], b * G + (g - 1))
                for n in range(GH):
                    m = pe.transpose(PB[g % 2][:, n * S:(n + 1) * S], P[:, g, n, :], ident[:])
                m.then_inc(z["pt_ready"], 1)

            def pv(b, g, par):
                wait(pe, z["pt_done"], b * G + (g + 1))
                wait(pe, z["v_done"], b + 1)
                for n in range(GH):
                    m = pe.matmul(PB[g % 2][:, n * (HD + 1):(n + 1) * (HD + 1)], PT[g % 2][:, n, :],
                                  vaug[par][:, g * GH + n, :], start=True, stop=True)
                m.then_inc(z["pv_ready"], 1)

            def step(i, par, half):
                attn, proj, tail = within(i, 0), within(i, 1), within(i, -1)
                q, qh = 1 - par, (half + 1 if par else half)
                th = half if par else half - 1
                if attn:
                    scores(i, 1)
                if within(i, -2):
                    t_rank(i - 2)
                if tail:
                    t_o(i - 1)
                    linger(i, last=3)
                if attn:
                    scores(i, 2)
                if proj:
                    p_xa(i + 1, q, qh)
                    if isinstance(i, int) and i == -1:
                        keep_busy(3, zeros[:, 0:128], zeros)
                if isinstance(i, int) and i == 1:
                    pe.wait_ge(s_rest, 32)
                if tail:
                    t_wo(i - 1)
                    linger(i, last=3)
                if attn:
                    scores(i, 3)
                    transp(i, 0)
                if proj:
                    p_h(i + 1, q)
                if tail:
                    t_x1T(i - 1, q)
                    linger(i, last=3)
                if attn:
                    pv(i, 0, par)
                if isinstance(i, int) and i == -1:
                    pe.wait_ge(s_wk, 32)
                linger(i, first=3)
                if proj:
                    wait(pe, z["h_done"], i + 2)
                    p_qk(i + 1, WkT, "k_ready")
                    linger(i, first=4)
                if attn:
                    transp(i, 1)
                if tail:
                    t_w2(i - 1, q, th)
                    linger(i, last=3)
                if isinstance(i, int) and i == -1:
                    pe.wait_ge(s_qv, 48)
                if proj:
                    wait(pe, z["k_done"], i + 2)
                    p_qk(i + 1, WqT, "q_ready")
                    linger(i, first=4)
                if attn:
                    pv(i, 1, par)
                if tail:
                    t_x2T(i - 1, q)
                    linger(i, last=3)
                if attn:
                    transp(i, 2)
                    linger(i, drain=2)
                if proj:
                    p_v(i + 1)
                if tail:
                    t_lg(i - 1)
                    linger(i, last=7)
                if attn:
                    pv(i, 2, par)
                    transp(i, 3)
                    linger(i, drain=4)
                if proj:
                    scores(i + 1, 0)
                if attn:
                    pv(i, 3, par)
                    linger(i, drain=4)

            steps(pe, -1, B + 2, 3, B - 1, step)

            keep_busy(2, onesb, causal)
            pe.wait_ge(z["selsum_done"], B + 1)
            pe.wait_ge(z["rank_done"], B)
            pe.matmul(M[1][:, 0:E], onesb[:], selsum[:], start=True, stop=True).then_inc(s_cnt, 1)

            keep_busy(8, onesb, causal)
            pe.wait_ge(s_plan, PLAN_TILES)
            for k in range(2):
                m = pe.matmul(M[0][0:1, k * 128:(k + 1) * 128], tile_of[:, k:k + 1], ident[:], start=True, stop=True)
            m.then_inc(s_planrow, 1)
            keep_busy(44, onesb, causal)

            pe.wait_ge(s_experts, 16 * 2 * E)
            pe.wait_ge(s_plan, PLAN)

            def xt(t, par, half):
                wait(pe, s_gathered[par], (half + 1) * 16)
                wait(pe, f["xgT_done"], t - 1)
                for c in range(C):
                    m = pe.transpose(XTB[par][:, c * 128:(c + 1) * 128], xg[par][:, c * 128:(c + 1) * 128], ident[:])
                m.then_inc(f["xgT_ready"], 1)

            def gate_up(t, par, e):
                wait(pe, f["xgT_done"], t + 1)
                wait(pe, f["gub_done"], t - 1)
                for c in range(C):
                    m = pe.matmul(GU[par][:], xgT[par][:, c * 128:(c + 1) * 128], We[:, bass.ds(e * WE + c * 2 * D, 2 * D)],
                                  start=(c == 0), stop=(c == C - 1))
                m.then_inc(f["gu_ready"], 1)

            def ht(t, par):
                wait(pe, f["hh_done"], t + 1)
                wait(pe, f["hhT_done"], t - 1)
                for c in range(C):
                    m = pe.transpose(HTB[par][:, c * 128:(c + 1) * 128], hh[par][:, c * 128:(c + 1) * 128], ident[:])
                m.then_inc(f["hhT_ready"], 1)

            def down(t, par, e):
                wait(pe, f["hhT_done"], t + 1)
                wait(pe, f["yb_done"], t - 1)
                for c in range(C):
                    m = pe.matmul(YB[par][:, 0:H], hhT[par][:, c * 128:(c + 1) * 128], We[:, bass.ds(e * WE + (C * 2 * D + c * H), H)],
                                  start=(c == 0), stop=(c == C - 1))
                m.then_inc(f["y_ready"], 1)

            def tstep(t, par, half, e_down, e_up):
                if within(t, 0, NT):
                    xt(t, par, half)
                if within(t, -3, NT):
                    down(t - 3, 1 - par, e_down)
                if within(t, -2, NT):
                    ht(t - 2, par)
                if within(t, 0, NT):
                    gate_up(t, par, e_up)

            tile_steps(pe, mybir.EngineType.PE, plan_p, E - 1, 1, (NT + 1) // 2, NT + 3, tstep)

        @block.scalar
        def _(act):
            act.wait_ge(s_first, 32)
            act.activation(scratch[:], small[:, 0:1], ACT.Exp)

            def evac(dst, src, ready, done, b, free, free_count):
                wait(act, z[ready], b + 1)
                wait(act, z[free], free_count)
                act.activation(dst, src, ACT.Copy).then_inc(z[done], 1)

            def exps(b, g, first=0, last=GH):
                if first == 0:
                    wait(act, z["max_done"], b * G + (g + 1))
                for n in range(first, last):
                    m = act.activation(P[:, g, n, :], P[:, g, n, :], ACT.Exp, bias=nmax[:, g, n:n + 1])
                if last == GH:
                    m.then_inc(z["exp_done"], 1)

            def pt(b, g):
                wait(act, z["pt_ready"], b * G + (g + 1))
                wait(act, z["pv_ready"], b * G + (g - 1))
                act.activation(PT[g % 2][:].rearrange("q h t -> q (h t)"), PB[g % 2][:], ACT.Copy)\
                    .then_inc(z["pt_done"], 1)

            def biased(dst, bias, ready, done, b):
                wait(act, z[ready], b + 1)
                for c in range(C):
                    m = act.activation(dst[:, c, :], M[1][:, c * S:(c + 1) * S], ACT.Identity, bias=bias[:, c:c + 1])
                m.then_inc(z[done], 1)

            def two(t):
                return t[:].rearrange("p c t -> p (c t)")

            def step(i, par, half):
                attn, proj, tail = within(i, 0), within(i, 1), within(i, -1)
                if tail:
                    evac(two(oT), M[0][:, 0:C * S], "oT_ready", "oT_done", i - 1, "x1_ready", i - 1)
                if attn:
                    exps(i, 0)
                    exps(i, 1)
                    pt(i, 0)
                    exps(i, 2, last=GH // 2)
                if proj:
                    evac(two(hT), M[1][:, 0:C * S], "h_ready", "h_done", i + 1, "v_ready", i + 1)
                if tail:
                    evac(two(x1T), M[0][:, 0:C * S], "x1T_ready", "x1T_done", i - 1, "x2_ready", i - 1)
                if attn:
                    exps(i, 2, first=GH // 2)
                if proj:
                    wait(act, z["km_done"], (i + 1) * C)
                    biased(kT, bk, "k_ready", "k_done", i + 1)
                if attn:
                    pt(i, 1)
                    exps(i, 3)
                if proj:
                    wait(act, z["scores_ready"], (i + 1) * G)
                    biased(qT, bq, "q_ready", "q_done", i + 1)
                if tail:
                    evac(two(x2T), M[0][:, 0:C * S], "x2T_ready", "x2T_done", i - 1, "lg_ready", i - 1)
                if attn:
                    pt(i, 2)
                    pt(i, 3)
                if tail:
                    wait(act, z["dtop_done"], i)
                    wait(act, z["pair_done"], i - 1)
                    act.activation(etop[:], dtop[:], ACT.Exp).then_inc(z["etop_done"], 1)

            steps(act, -1, B + 1, 3, B - 1, step)
            act.activation(scratch[:], small[:, 0:1], ACT.Sigmoid)

            def xt_out(t, par):
                wait(act, f["xgT_ready"], t + 1)
                wait(act, f["gu_ready"], t - 1)
                act.activation(xgT[par], XTB[par][:, 0:C * 128], ACT.Copy).then_inc(f["xgT_done"], 1)

            def tstep(t, par, half):
                q = 1 - par
                if within(t, 0, NT):
                    wait(act, f["gclip_done"], t + 1)
                    wait(act, f["hh_done"], t - 1)
                    act.activation(sg[par][:], gu[par][:, 0, :], ACT.Sigmoid, scale=ALPHA).then_inc(f["sig_done"], 1)
                if within(t, -1, NT):
                    wait(act, f["hhT_ready"], t)
                    wait(act, f["y_ready"], t - 2)
                    act.activation(hhT[q], HTB[q][:, 0:C * 128], ACT.Copy).then_inc(f["hhT_done"], 1)
                if within(t, -2, NT):
                    wait(act, f["yb_done"], t - 1)
                    wait(act, f["ids_done"], t - 1)
                    wait(act, s_added, (t - 3) * 16)
                    act.activation(yw[par][:], yb[par][:], ACT.Copy, scale=ids[par][:, 1:2].bitcast(F32))\
                        .then_inc(f["yw_done"], 1)
                if within(t, 2, NT):
                    xt_out(t + 2, par)

            xt_out(0, 0)
            xt_out(1, 1)
            steps(act, 0, NT + 2, 6, NT - 3, tstep)

        @block.vector
        def _(dve):
            dve.memset(zeros[:], 0.0).then_inc(s_zeros, 1)
            dve.memset(selsum[:], 0.0).then_inc(z["selsum_done"], 1)
            for i in range(2):
                last = dve.memset(vaug[i][:, :, HD:HD + 1], 1.0)
            dve.memset(one_e[:], 1.0).then_inc(s_init, 1)
            dve.wait_ge(s_first, 32)

            def heads(ap):
                return ap.rearrange("q (h d) -> q h d", h=NH)

            def masked(b, g):
                wait(dve, z["scores_ready"], b * G + (g + 1))
                wait(dve, z["pt_ready"], (b - 1) * G + (g + 1))
                dve.tensor_tensor(out=P[:, g], in0=SC[g][:].rearrange("q (h t) -> q h t", h=GH),
                                  in1=causal.rearrange("q (h t) -> q h t", h=GH), op=ALU.add).then_inc(z["mask_done"], 1)

            def maximum(b, g):
                wait(dve, z["mask_done"], b * G + (g + 1))
                dve.tensor_reduce(out=nmax[:, g], in_=P[:, g], axis=AX.X, op=ALU.max, negate=True).then_inc(z["max_done"], 1)

            def softmax(b, g):
                masked(b, g)
                maximum(b, g)

            def norm(b, g):
                wait(dve, z["pv_ready"], b * G + (g + 1))
                pvo = PB[g % 2][:, 0:GH * (HD + 1)].rearrange("q (n d) -> q n d", d=HD + 1)
                dve.reciprocal(rsum[:, g % 2, :], pvo[:, :, HD]).then_inc(z["rsum_done"], 1)
                wait(dve, z["rsum_done"], b * G + (g + 1))
                wait(dve, z["oT_ready"], b)
                dve.tensor_tensor(out=o[:, g * GH:(g + 1) * GH, :], in0=pvo[:, :, 0:HD],
                                  in1=rsum[:, g % 2, :].unsqueeze(2).broadcast_to([S, GH, HD]), op=ALU.mult)\
                    .then_inc(z["norm_done"], 1)

            def x1_out(b, par, half):
                wait(dve, z["x1_ready"], b + 1)
                wait(dve, z["xb_done"], b + 1)
                wait(dve, s_x1_stored[par], half * 16)
                wait(dve, z["x1T_ready"], b - 1)
                dve.tensor_tensor(out=x1[par][:], in0=M[1][:, 0:H], in1=xb[:], op=ALU.add).then_inc(z["x1_done"], 1)

            def x2_out(b, par, half):
                wait(dve, z["x2_ready"], b + 1)
                wait(dve, s_x2_stored[par], half * 16)
                wait(dve, s_late[par], (half + 1) * 48)
                wait(dve, z["x2T_ready"], b - 1)
                dve.tensor_tensor(out=x2[par][:], in0=M[0][:, 0:H], in1=b2[par][:], op=ALU.add).then_inc(z["x2_done"], 1)

            def xa_out(b, par, half):
                wait(dve, z["xa_ready"], b + 1)
                wait(dve, s_early[par], (half + 1) * 48)
                wait(dve, z["h_ready"], b)
                dve.tensor_scalar(out=xa[:], in0=M[0][0:RANK, 0:S], scalar1=BT[par][:, H:H + 1], scalar2=None, op0=ALU.mult)\
                    .then_inc(z["xa_done"], 1)

            def v_out(b, par):
                wait(dve, z["v_ready"], b + 1)
                wait(dve, z["pv_ready"], (b - 1) * G)
                dve.tensor_tensor(out=vaug[par][:, :, 0:HD], in0=heads(M[1][:, 0:H]), in1=heads(bv[:]), op=ALU.add)\
                    .then_inc(z["v_done"], 1)

            def choose(b):
                wait(dve, z["lg_ready"], b + 1)
                dve.tensor_tensor(out=lg[:], in0=M[0][:, 0:E], in1=rbias[:], op=ALU.add).then_inc(z["lg_done"], 1)
                stand_alone(dve, (z["lg_done"], b + 1), (z["etop_done"], b))
                dve.max(out=top8[:], in_=lg[:]).then_inc(z["top_done"], 1)
                stand_alone(dve, (z["top_done"], b + 1))
                dve.max_index(out=topi[:], in_max=top8[:], in_values=lg[:]).then_inc(z["topi_done"], 1)
                dve.tensor_scalar(out=dtop[:], in0=top8[:, 0:TOPK], scalar1=top8[:, 0:1], scalar2=None, op0=ALU.subtract)\
                    .then_inc(z["dtop_done"], 1)
                wait(dve, z["topi_done"], b + 1)
                dve.tensor_copy(topf[:], topi[:, 0:TOPK]).then_inc(z["topf_done"], 1)
                wait(dve, z["topf_done"], b + 1)
                dve.tensor_tensor(out=onehot[:], in0=topf[:].unsqueeze(2).broadcast_to([S, TOPK, E]),
                                  in1=iota_e[:].unsqueeze(1).broadcast_to([S, TOPK, E]), op=ALU.is_equal)\
                    .then_inc(z["onehot_done"], 1)
                wait(dve, z["onehot_done"], b + 1)
                wait(dve, z["rank_ready"], b)
                with nc.allow_low_precision(reason="ones and zeros"):
                    dve.tensor_reduce(out=sel[:], in_=onehot[:].rearrange("p j e -> p e j"), axis=AX.X, op=ALU.add)\
                        .then_inc(z["sel_done"], 1)

            def ranked(b):
                wait(dve, z["rank_ready"], b + 1)
                dve.tensor_tensor(out=rank[:], in0=M[1][:, 0:E], in1=ebase[:], op=ALU.add).then_inc(z["rank_done"], 1)
                dve.tensor_tensor(out=selsum[:], in0=selsum[:], in1=sel[:], op=ALU.add).then_inc(z["selsum_done"], 1)

            def place(b, par, half):
                wait(dve, z["rank_done"], b + 1)
                dve.tensor_tensor(out=prod[:], in0=onehot[:], in1=rank[:].unsqueeze(1).broadcast_to([S, TOPK, E]),
                                  op=ALU.mult).then_inc(z["prod_done"], 1)
                wait(dve, z["etop_done"], b + 1)
                dve.tensor_reduce(out=esum[:], in_=etop[:], axis=AX.X, op=ALU.add).then_inc(z["esum_done"], 1)
                wait(dve, z["prod_done"], b + 1)
                with nc.allow_low_precision(reason="whole numbers below 2^24"):
                    dve.tensor_reduce(out=slot[:], in_=prod[:], axis=AX.X, op=ALU.add).then_inc(z["slot_done"], 1)
                wait(dve, z["esum_done"], b + 1)
                dve.reciprocal(einv[:], esum[:]).then_inc(z["einv_done"], 1)
                wait(dve, z["slot_done"], b + 1)
                dve.tensor_scalar(out=slot_p[:], in0=slot[:], scalar1=127, scalar2=None, op0=ALU.bitwise_and)\
                    .then_inc(z["slotp_done"], 1)
                dve.tensor_scalar(out=slot_c[:], in0=slot[:], scalar1=7, scalar2=None, op0=ALU.arith_shift_right)\
                    .then_inc(z["slotc_done"], 1)
                wait(dve, s_scattered[par], half * (16 * TOPK))
                wait(dve, z["einv_done"], b + 1)
                dve.tensor_scalar(out=pair[par][:, :, 1].bitcast(F32), in0=etop[:], scalar1=einv[:, 0:1], scalar2=None,
                                  op0=ALU.mult)
                dve.tensor_scalar(out=pair[par][:, :, 0], in0=pair[par][:, :, 0], scalar1=float(2 * S), scalar2=None,
                                  op0=ALU.add).then_inc(z["pair_done"], 1)
                wait(dve, z["slotp_done"], b + 1)
                wait(dve, z["slotc_done"], b + 1)
                dve.scalar_tensor_tensor(out=slot_row[par][:], in0=slot_p[:], scalar=float(TCOLS), in1=slot_c[:],
                                         op0=ALU.mult, op1=ALU.add).then_inc(z["slotrow_done"], 1)

            def step(i, par, half):
                attn, proj, tail = within(i, 0), within(i, 1), within(i, -1)
                q, qh = 1 - par, (half + 1 if par else half)
                th = half if par else half - 1
                if within(i, -2):
                    ranked(i - 2)
                if attn:
                    softmax(i, 1)
                if proj:
                    xa_out(i + 1, q, qh)
                if attn:
                    masked(i, 2)
                if tail:
                    x1_out(i - 1, q, th)
                if attn:
                    maximum(i, 2)
                    softmax(i, 3)
                if isinstance(i, int) and i == 2:
                    dve.wait_ge(s_rest, 32)
                if within(i, -2):
                    place(i - 2, par, half - 1)
                if attn:
                    norm(i, 0)
                if tail:
                    x2_out(i - 1, q, th)
                if attn:
                    norm(i, 1)
                if tail:
                    choose(i - 1)
                if isinstance(i, int) and i == -1:
                    dve.wait_ge(s_qv, 48)
                if proj:
                    v_out(i + 1, q)
                if attn:
                    norm(i, 2)
                if proj:
                    masked(i + 1, 0)
                if attn:
                    norm(i, 3)
                if proj:
                    maximum(i + 1, 0)

            steps(dve, -1, B + 2, 5, B - 1, step)

            dve.wait_ge(s_cnt, 1)
            n = [0]

            def then(m):
                m.then_inc(s_plan, 1)
                n[0] += 1
                dve.wait_ge(s_plan, n[0])

            then(dve.tensor_scalar(out=cnt[:], in0=M[1][:, 0:E], scalar1=127.0, scalar2=None, op0=ALU.add))
            then(dve.tensor_scalar(out=ntile[:], in0=cnt[:], scalar1=7, scalar2=None, op0=ALU.arith_shift_right))
            then(dve.tensor_copy(ntilef[:], ntile[:]))
            then(dve.tensor_tensor_scan(out=cum[:], data0=one_e[:], data1=ntilef[:], initial=0.0, op0=ALU.mult, op1=ALU.add))
            then(dve.tensor_scalar(out=past[:], in0=cum[:], scalar1=tile_id[:, 0:1], scalar2=None, op0=ALU.is_le))
            then(dve.tensor_reduce(out=t_e[:], in_=past[:], axis=AX.X, op=ALU.add))
            then(dve.tensor_tensor(out=past[:], in0=past[:], in1=ntilef[:], op=ALU.mult))
            then(dve.tensor_reduce(out=t_s[:], in_=past[:], axis=AX.X, op=ALU.add))
            then(dve.scalar_tensor_tensor(out=t_r[:], in0=t_e[:], scalar=float(RT), in1=tile_id, op0=ALU.mult, op1=ALU.add))
            then(dve.tensor_tensor(out=t_r[:], in0=t_r[:], in1=t_s[:], op=ALU.subtract))
            then(dve.tensor_scalar(out=tile_of[:, 0:1], in0=t_e[:], scalar1=float(E - 1), scalar2=0.0, op0=ALU.min, op1=ALU.max))
            then(dve.tensor_scalar(out=tile_of[:, 1:2], in0=t_r[:], scalar1=float(TCOLS - 1), scalar2=0.0,
                                   op0=ALU.min, op1=ALU.max))
            assert n[0] == PLAN_TILES
            dve.wait_ge(s_planrow, 1)
            for plan, row, first, later in ((plan_c, M[0][0:1, 128:256], 2, 7), (plan_p, M[0][0:1, 0:128], 0, 3),
                                            (plan_e, M[0][0:1, 0:128], 2, 4)):
                rows = plan[:].rearrange("p (k four) -> p k four", four=4)
                n_rows = plan.shape[1] // 4
                for at, begin in ((0, first), (2, later)):
                    dve.tensor_copy(rows[:, :, at:at + 2],
                                    row[:, begin:begin + 2 * n_rows].rearrange("p (k two) -> p k two", two=2))\
                        .then_inc(s_plan, 1)
                    n[0] += 1
            assert n[0] == PLAN
            dve.wait_ge(s_plan, PLAN)

            dve.wait_ge(s_experts, 16 * 2 * E)

            def tstep(t, par, half, e_down, e_up):
                if within(t, 0, NT):
                    wait(dve, f["gu_ready"], t + 1)
                    g2 = gu[par][:].rearrange("p k d -> p (k d)")
                    dve.tensor_tensor(out=g2, in0=GU[par][:], in1=be[:, bass.ds(e_up * BE, 2 * D)], op=ALU.add)\
                        .then_inc(f["gub_done"], 1)
                    wait(dve, f["gub_done"], t + 1)
                    dve.tensor_scalar(out=gu[par][:, 0, :], in0=gu[par][:, 0, :], scalar1=LIMIT, scalar2=None, op0=ALU.min)\
                        .then_inc(f["gclip_done"], 1)
                    dve.tensor_scalar(out=gu[par][:, 1, :], in0=gu[par][:, 1, :], scalar1=LIMIT, scalar2=-LIMIT,
                                      op0=ALU.min, op1=ALU.max).then_inc(f["uclip_done"], 1)
                if within(t, -2, NT):
                    wait(dve, f["y_ready"], t - 1)
                    wait(dve, f["yw_done"], t - 3)
                    dve.tensor_tensor(out=yb[par][:], in0=YB[par][:, 0:H], in1=be[:, bass.ds(e_down * BE + 2 * D, H)], op=ALU.add)\
                        .then_inc(f["yb_done"], 1)
                if within(t, 0, NT):
                    wait(dve, f["sig_done"], t + 1)
                    dve.tensor_tensor(out=sg[par][:], in0=sg[par][:], in1=gu[par][:, 0, :], op=ALU.mult)\
                        .then_inc(f["glu_done"], 1)
                    wait(dve, f["glu_done"], t + 1)
                    wait(dve, f["uclip_done"], t + 1)
                    wait(dve, f["hhT_ready"], t - 1)
                    dve.scalar_tensor_tensor(out=hh[par][:], in0=gu[par][:, 1, :], scalar=1.0, in1=sg[par][:],
                                             op0=ALU.add, op1=ALU.mult).then_inc(f["hh_done"], 1)

            tile_steps(dve, mybir.EngineType.DVE, plan_e, E - 1, 0, (NT - 1) // 2, NT + 2, tstep)


FIRST_C = (4, 5, 8)
PLAN_TILES = 12
PLAN = 18


def kernel(**inputs):
    import numpy as np
    import ml_dtypes
    import concourse.bacc as bacc
    from concourse.bass_utils import run_bass_kernel_spmd

    v = {k: np.asarray(x) for k, x in inputs.items()}
    bf = ml_dtypes.bfloat16

    def chunked(w):
        return w.reshape(-1, 128, w.shape[-1]).transpose(1, 0, 2)

    def chunks_aside(w):
        return w.reshape(E, -1, 128, w.shape[-1]).transpose(0, 2, 1, 3).reshape(E, 128, -1)

    def apart(w):
        return np.concatenate([w[..., ::2], w[..., 1::2]], -1)

    p = np.arange(128)
    q, k = p[:, None], p[None, :]
    mask = np.where(k <= q, 0.0, -2.0 ** 100)
    table = np.zeros((128, TCOLS, 2), np.int32)
    table[:, :, 0] = ROWS + q
    pair = np.zeros((2, 128, TOPK, 2), np.int32)
    pair[:, :, :, 0] = (p[:, None] + 128 * np.arange(2)[:, None, None] - 2 * S)
    arrays = {
        "idx": np.concatenate([v["itok_B_0_6"], v["itok_B_0_15"]]).reshape(1, 2 * B),
        "xT": v["x"].reshape(B, S, C, 128).transpose(0, 3, 2, 1),
        "x": v["x"],
        "AT": v["L0_cond_A"].reshape(8, RANK, C, 128).transpose(0, 3, 2, 1),
        "BT": np.concatenate([v["L0_cond_Bm"].transpose(0, 2, 1),
                              np.tile(v["L0_cond_scalings"][:, None, None], (1, RANK, 1))], -1),
        "W2": v["L0_cond2_W"].reshape(E, C, 128, H).transpose(0, 2, 1, 3),
        "b2": v["L0_cond2_b"],
        "WT": chunked(v["L0_cond_W"].T),
        "WqT": chunked(v["L0_attn_Wq"].T),
        "WkT": chunked(v["L0_attn_Wk"].T),
        "WvT": chunked(v["L0_attn_Wv"].T),
        "WoT": chunked(v["L0_attn_Wo"].T),
        "biases": np.concatenate([v["L0_attn_bv"], v["L0_attn_bo"], v["L0_ffn_router_bias"]]),
        "experts": np.concatenate([chunks_aside(apart(v["L0_ffn_gate_up_proj"])), chunks_aside(v["L0_ffn_down_proj"])], -1),
        "expert_biases": np.concatenate([apart(v["L0_ffn_gate_up_proj_bias"]), v["L0_ffn_down_proj_bias"]], -1),
        "small": np.concatenate([
            np.eye(128, dtype=np.float32),
            np.tile(np.arange(E, dtype=np.float32), (128, 1)),
            np.tile(np.arange(E, dtype=np.float32) * ROWS, (128, 1)),
            (p[:, None] // HD == np.arange(CH)).astype(np.float32) / np.float32(HD ** 0.5),
            v["L0_attn_bq"].reshape(C, 128).T,
            v["L0_attn_bk"].reshape(C, 128).T,
            chunked(v["L0_ffn_router_weight"].T).reshape(128, -1),
            p[:, None].astype(np.float32) - 4], -1),
        "patterns": np.concatenate([np.tile(mask, (1, GH)), q < k, np.ones((128, 128))], -1).astype(bf),
        "table": table.reshape(128, -1),
        "pairs": np.concatenate([pair[0].reshape(128, -1), pair[1].reshape(128, -1)], -1),
    }
    nc = bacc.Bacc("TRN2", target_bir_lowering=False, num_devices=1)
    feeds, aps = {}, {}
    for name, arr in arrays.items():
        arr = np.ascontiguousarray(arr)
        feeds[f"in_{name}"] = arr
        aps[name] = nc.dram_tensor(f"in_{name}", arr.shape, mybir.dt.from_np(arr.dtype), kind="ExternalInput").ap()
    out = nc.dram_tensor("out_rows", (ROWS + PADROWS, H), F32, kind="ExternalOutput").ap()
    adaln_attn_moe(nc, aps, out)
    r = run_bass_kernel_spmd(nc, [feeds], core_ids=[0])
    return r.results[0]["out_rows"][:ROWS].reshape(B, S, H)
```
